# Optimizing a Trainium2 kernel written in Bass

```python
import numpy as np
import jax
import jax.numpy as jnp

def _softmax(x, axis=-1):
    return jax.nn.softmax(x, axis=axis)

def _gelu(x):
    return jax.nn.gelu(x, approximate=True)

def _silu(x):
    return jax.nn.silu(x)

def _sigmoid(x):
    return jax.nn.sigmoid(x)

def _layernorm(x, axis=-1, eps=1e-05):
    m = jnp.mean(x, axis=axis, keepdims=True)
    v = jnp.var(x, axis=axis, keepdims=True)
    return (x - m) / jnp.sqrt(v + eps)

def _scatter_add(tgt, idx, src, axis=0):
    return tgt.at[idx].add(src)

def _segment_sum(src, seg, n):
    return jax.ops.segment_sum(src, seg, n)
kernel_name = 'mk_seq_preln_d1_jaxref_r8_1fc711'

def setup_inputs(seed: int=0):
    np.random.seed(seed)
    _w = jnp.asarray

    def _L0_attn_setup():
        import jax, jax.numpy as jnp
        import numpy as np
        B, S, D_MODEL, D_K = (4, 256, 128, 1)
        D_QKV = D_MODEL * D_K
        MASK_NEG = -9000000000000000.0

        def _scaled_dot_product_attention(q, k, v):
            d_k = k.shape[-1]
            scores = jnp.einsum('bqd,bkd->bqk', q, k) / jnp.sqrt(jnp.float32(d_k))
            scores = jnp.triu(scores, k=0)
            scores = jnp.where(scores == 0, MASK_NEG, scores)
            attn = jax.nn.softmax(scores, axis=-1)
            return jnp.einsum('bqk,bkd->bqd', attn, v)
        key = jax.random.key(seed)
        kx, kw = jax.random.split(key)
        x = jax.random.normal(kx, (B, S, D_MODEL), dtype=jnp.float32)
        W = jax.random.normal(kw, (D_MODEL, 3 * D_QKV), dtype=jnp.float32) * (1.0 / np.sqrt(D_MODEL))
        return {'x': x, 'W': W}
    _L0_attn_in = _L0_attn_setup()

    def _L0_ffn_setup():
        import jax, jax.numpy as jnp
        import numpy as np
        D_MODEL = 128
        FFN_DIM = 256
        NUM_EXPERTS = 8
        NUM_GROUPS = 4
        EXPERTS_PER_GROUP = NUM_EXPERTS // NUM_GROUPS
        TOP_K = 2
        GROUPS_TOP_K = 1
        EPS = 1e-09

        def _topk_normalized(scores, k):
            vals, idx = jax.lax.top_k(scores, k)
            vals = vals / (jnp.sum(vals, axis=-1, keepdims=True) + EPS)
            return (vals, idx)
        key = jax.random.key(seed)
        ks = jax.random.split(key, 6)
        B, S = (2, 128)
        x = jax.random.normal(ks[0], (B, S, D_MODEL), dtype=jnp.float32)
        sd = 0.02
        macro_w = jax.random.normal(ks[1], (D_MODEL, NUM_GROUPS), dtype=jnp.float32) * sd
        micro_w = jax.random.normal(ks[2], (NUM_GROUPS, D_MODEL, EXPERTS_PER_GROUP), dtype=jnp.float32) * sd
        gate_w = jax.random.normal(ks[3], (NUM_EXPERTS, D_MODEL, FFN_DIM), dtype=jnp.float32) * sd
        up_w = jax.random.normal(ks[4], (NUM_EXPERTS, D_MODEL, FFN_DIM), dtype=jnp.float32) * sd
        down_w = jax.random.normal(ks[5], (NUM_EXPERTS, FFN_DIM, D_MODEL), dtype=jnp.float32) * sd
        return {'x': x, 'macro_w': macro_w, 'micro_w': micro_w, 'gate_w': gate_w, 'up_w': up_w, 'down_w': down_w}
    _L0_ffn_in = _L0_ffn_setup()
    _d = {'L0_attn_x': _L0_attn_in['x'], 'L0_attn_W': _L0_attn_in['W'], 'L0_ffn_macro_w': _L0_ffn_in['macro_w'], 'L0_ffn_micro_w': _L0_ffn_in['micro_w'], 'L0_ffn_gate_w': _L0_ffn_in['gate_w'], 'L0_ffn_up_w': _L0_ffn_in['up_w'], 'L0_ffn_down_w': _L0_ffn_in['down_w']}
    _x0 = _d['L0_attn_x']
    _d['L0_attn_x'] = jax.random.normal(jax.random.fold_in(jax.random.key(seed), 1), (16, 512, 128), dtype=_x0.dtype)
    del _x0
    return _d

def reference(L0_attn_x, L0_attn_W, L0_ffn_macro_w, L0_ffn_micro_w, L0_ffn_gate_w, L0_ffn_up_w, L0_ffn_down_w):

    def _L0_attn_ref(x, W):
        import jax, jax.numpy as jnp
        import numpy as np
        B, S, D_MODEL, D_K = (4, 256, 128, 1)
        D_QKV = D_MODEL * D_K
        MASK_NEG = -9000000000000000.0

        def _scaled_dot_product_attention(q, k, v):
            d_k = k.shape[-1]
            scores = jnp.einsum('bqd,bkd->bqk', q, k) / jnp.sqrt(jnp.float32(d_k))
            scores = jnp.triu(scores, k=0)
            scores = jnp.where(scores == 0, MASK_NEG, scores)
            attn = jax.nn.softmax(scores, axis=-1)
            return jnp.einsum('bqk,bkd->bqd', attn, v)
        qkv = jnp.einsum('bsd,df->bsf', x, W)
        q, k, v = jnp.split(qkv, 3, axis=-1)
        return _scaled_dot_product_attention(q, k, v)

    def _L0_ffn_ref(x, macro_w, micro_w, gate_w, up_w, down_w):
        import jax, jax.numpy as jnp
        import numpy as np
        D_MODEL = 128
        FFN_DIM = 256
        NUM_EXPERTS = 8
        NUM_GROUPS = 4
        EXPERTS_PER_GROUP = NUM_EXPERTS // NUM_GROUPS
        TOP_K = 2
        GROUPS_TOP_K = 1
        EPS = 1e-09

        def _topk_normalized(scores, k):
            vals, idx = jax.lax.top_k(scores, k)
            vals = vals / (jnp.sum(vals, axis=-1, keepdims=True) + EPS)
            return (vals, idx)
        B, S, D = x.shape
        T = B * S
        xf = x.reshape(T, D)
        macro_scores = jax.nn.sigmoid(xf @ macro_w)
        mv, mi = _topk_normalized(macro_scores, GROUPS_TOP_K)
        macro_full = jnp.sum(jax.nn.one_hot(mi, NUM_GROUPS, dtype=xf.dtype) * mv[..., None], axis=1)
        micro_scores = jax.nn.sigmoid(jnp.einsum('td,gde->tge', xf, micro_w))
        uv, ui = _topk_normalized(micro_scores, TOP_K)
        micro_full = jnp.sum(jax.nn.one_hot(ui, EXPERTS_PER_GROUP, dtype=xf.dtype) * uv[..., None], axis=2)
        w = (macro_full[:, :, None] * micro_full).reshape(T, NUM_EXPERTS)
        gate = jax.nn.silu(jnp.einsum('td,edf->tef', xf, gate_w))
        up = jnp.einsum('td,edf->tef', xf, up_w)
        h = gate * up
        out = jnp.einsum('te,tef,efd->td', w, h, down_w)
        return out.reshape(B, S, D)
    x = L0_attn_x
    x = x + _L0_attn_ref(_layernorm(x, axis=-1), L0_attn_W)
    x = x + _L0_ffn_ref(_layernorm(x, axis=-1), L0_ffn_macro_w, L0_ffn_micro_w, L0_ffn_gate_w, L0_ffn_up_w, L0_ffn_down_w)
    return x

_drawn_inputs = setup_inputs


def setup_inputs(seed=0):
    import zlib

    import numpy as np

    out = dict(_drawn_inputs(seed))
    spreads = {}
    factors = {'L0_ffn_macro_w': 8.0,
     'L0_ffn_micro_w': 8.0,
     'L0_ffn_gate_w': 8.0,
     'L0_ffn_up_w': 8.0,
     'L0_ffn_down_w': 8.0}
    for name, (base, spread) in spreads.items():
        noise = np.random.default_rng([zlib.crc32(name.encode()), seed]).standard_normal(out[name].shape)
        drawn = base * np.exp(spread * noise) if base else spread * noise
        out[name] = jnp.asarray(drawn.astype(out[name].dtype))
    for name, factor in factors.items():
        out[name] = (out[name] * factor).astype(out[name].dtype)
    return out
```

```python
import concourse.bass as bass
from concourse import mybir
from contextlib import ExitStack

F32 = mybir.dt.float32
F32R = mybir.dt.float32r
BF16 = mybir.dt.bfloat16
F16 = mybir.dt.float16
I32 = mybir.dt.int32
ALU = mybir.AluOpType
ACT = mybir.ActivationFunctionType
AX = mybir.AxisListType

P = 128


class Turn:

    def __init__(self, ring, trip, off):
        self.ring, self.trip, self.off = ring, trip, off
        self.buf = off % ring
        self.number = off if isinstance(trip, int) else ring * trip + off
        self.round = off // ring if isinstance(trip, int) else trip + off // ring

    def __add__(self, d):
        return Turn(self.ring, self.trip, self.off + d)

    def __sub__(self, d):
        return self + -d

    def has(self, earlier):
        return not isinstance(self.trip, int) or self.off >= earlier

    def count(self, per, more):
        return self.number * per + more


def preln_attention_moe_kernel(nc, x_d, w_d, macro_d, micro_d, gate_d, up_d, down_d, out_d):
    B, S, D = x_d.shape
    NT = S // P
    T = B * S
    G, _, EPG = micro_d.shape
    F = gate_d.shape[2]
    EF = EPG * F
    NC = EF // P
    NL = G + G * EPG
    SCALE = 1.0 / float(D) ** 0.5
    MASKED = -2.0 ** 53
    ALL_MASKED = 1e14
    LN_EPS, TOP_EPS = 1e-5, 1e-9
    WIDTH = [S - P * i for i in range(NT)]
    OFF = [sum(WIDTH[:i]) for i in range(NT)]
    SW = sum(WIDTH)
    NEGMEAN, RSTD, WGT, TOKEN, RW = D, D + 1, D + 2, D + 4, D + 8
    REGION = T + P
    SLOTS = T // P + G - 1
    ROWS = G * REGION + (G - 1) * P
    R1 = 3
    R2 = 8
    STEPS = [list(range(-1, 6)), (2, 5), list(range(15, 20))]
    assert B == 16 and NT == 4 and R1 * 5 + 1 == B and SLOTS == 67

    scratch = nc.dram_tensor("sorted_rows", [ROWS, RW], F32).ap()

    ctx = ExitStack()
    with ctx:
        def sb(name, shape, dt=F32):
            return ctx.enter_context(nc.sbuf_tensor(name, shape, dt))

        def sem(name):
            return ctx.enter_context(nc.semaphore(name))

        ident = sb("ident", [P, P])
        identb = sb("identb", [P, P], BF16)
        trineg = sb("trineg", [P, P], BF16)
        before = sb("before", [P, P], F16)
        ones = sb("ones", [P, P], F16)
        halfneg = sb("halfneg", [P, NT])
        prefer = sb("prefer", [P, NT, G])
        partno = sb("partno", [P, G])
        padrow = sb("padrow", [P, RW])
        wqkv = sb("wqkv", [P, 3 * D])
        wqT = sb("wqT", [P, D])
        wkT = sb("wkT", [P, D])
        wqk = sb("wqk", [P, D])
        wrout = sb("wrout", [P, NL])
        wgu = sb("wgu", [P, G, 2 * EF])
        wguh = sb("wguh", [P, G, 2 * EF], F32R)
        wgul = sb("wgul", [P, G, 2 * EF], F32R)
        wd = sb("wd", [P, G, NC * D])
        wdh = sb("wdh", [P, G, NC * D], F32R)
        wdl = sb("wdl", [P, G, NC * D], F32R)
        xin = [sb(f"xin{r}", [P, NT, D]) for r in range(R1)]
        xres = [sb(f"xres{r}", [P, NT, D]) for r in range(R1)]
        st1 = sb("st1", [P, NT, 6])
        meanvar1 = sb("meanvar1", [P, NT, 2])
        vareps1 = sb("vareps1", [P, NT])
        norm1s = [sb(f"norm1s{r}", [P, NT, 2]) for r in range(R1)]
        xn = [sb(f"xn{r}", [P, NT, D]) for r in range(R1)]
        xnT = [sb(f"xnT{r}", [P, S]) for r in range(R1)]
        xsum = [sb(f"xsum{r}", [P, 1]) for r in range(R1)]
        qT = [sb(f"qT{r}", [P, S]) for r in range(R1)]
        zmask = [sb(f"zmask{r}", [P, S]) for r in range(2)]
        negs = [sb(f"negs{r}", [P, S]) for r in range(2)]
        negmax = [sb(f"negmax{r}", [P, NT]) for r in range(R1)]
        probs = [sb(f"probs{r}", [P, SW]) for r in range(R1)]
        psums = [sb(f"psums{r}", [P, NT]) for r in range(R1)]
        probsT = [sb(f"probsT{m}", [P, S]) for m in range(NT)]
        zT = sb("zT", [P, S])
        vtot = [sb(f"vtot{r}", [P, D]) for r in range(R1)]
        u512 = [sb(f"u512_{r}", [P, NT]) for r in range(R1)]
        resid = [sb(f"resid{r}", [P, NT, D]) for r in range(R1)]
        rsum = sb("rsum", [P, NT])
        rlive = sb("rlive", [P, NT])
        row = [sb(f"row{r}", [P, NT, RW]) for r in range(R1)]
        st2 = sb("st2", [P, NT, 6])
        meanvar2 = sb("meanvar2", [P, NT, 2])
        vareps2 = sb("vareps2", [P, NT])
        xn2 = [sb(f"xn2_{r}", [P, NT, D]) for r in range(R1)]
        x2T = sb("x2T", [P, S])
        elog = sb("elog", [P, NT, NL])
        elog1 = sb("elog1", [P, NT, NL])
        sig = sb("sig", [P, NT, NL])
        top = sb("top", [P, NT])
        istop = sb("istop", [P, NT, G])
        rank = sb("rank", [P, NT, G])
        toprank = sb("toprank", [P, NT])
        pick = [sb(f"pick{r}", [P, NT, G], F16) for r in range(R1)]
        micro = sb("micro", [P, NT, G, EPG])
        msel = sb("msel", [P, NT, EPG])
        msum = sb("msum", [P, NT])
        tope = sb("tope", [P, NT])
        wden = sb("wden", [P, NT])
        wrec = sb("wrec", [P, NT])
        wtop = sb("wtop", [P, NT])
        pairs = sb("pairs", [P, 2, G], F16)
        four = sb("four", [P, G], F16)
        carry = [sb(f"carry{r}", [P, G], F16) for r in range(R1)]
        posm = sb("posm", [P, NT, G])
        place = [sb(f"place{r}", [P, NT], I32) for r in range(R1)]
        ends = sb("ends", [P, G])
        padat = sb("padat", [P, G], I32)
        tileat = sb("tileat", [1, G, T // P])
        tilehit = sb("tilehit", [1, G, T // P])
        tiles = sb("tiles", [1, G])
        tcum = sb("tcum", [1, G])
        skip = sb("skip", [1, G])
        slotno = sb("slotno", [1, G, SLOTS])
        past = sb("past", [1, G, SLOTS])
        pastskip = sb("pastskip", [1, G, SLOTS])
        grp_f = sb("grp_f", [1, SLOTS])
        rowsum = sb("rowsum", [1, SLOTS])
        slot_group = sb("slot_group", [1, SLOTS], I32)
        slot_row = sb("slot_row", [1, SLOTS], I32)
        rowin = [sb(f"rowin{r}", [P, RW]) for r in range(R2)]
        yn = [sb(f"yn{r}", [P, D]) for r in range(R2)]
        yh = [sb(f"yh{r}", [P, P], F32R) for r in range(2)]
        yl = [sb(f"yl{r}", [P, P], F32R) for r in range(2)]
        act_g = [sb(f"act_g{r}", [P, EF]) for r in range(2)]
        hid = [sb(f"hid{r}", [P, EF]) for r in range(2)]
        hh = [sb(f"hh{r}", [P, EF], F32R) for r in range(2)]
        hl = [sb(f"hl{r}", [P, EF], F32R) for r in range(2)]
        outb = [sb(f"outb{r}", [P, D]) for r in range(R2)]

        bank = [ctx.enter_context(nc.psum_tensor(f"bank{i}", [P, 512], F32)) for i in range(8)]
        ps_tr, ps_z, ps_o, ps_m = bank[0], bank[1], bank[6], bank[7]
        ps_s, ps_pt = bank[2:4], bank[4:6]
        ps_vtot = ps_m[:, 0:D]
        ps_log = ps_m[:, D:D + NT * NL].rearrange("p (i l) -> p i l", l=NL)
        ps_pos = ps_m[:, 192:192 + NT * G].rearrange("p (i g) -> p i g", g=G)
        ps_end = ps_m[:, 256:256 + G]
        ps_y, ps_g, ps_u, ps_ht, ps_out = bank[0], bank[1:3], bank[3:5], bank[5], bank[6]

        w_in = sem("w_in")
        r_in = sem("r_in")
        e_in = sem("e_in")
        pad_out = sem("pad_out")
        x_in = [sem(f"x_in{r}") for r in range(R1)]
        res_in = [sem(f"res_in{r}") for r in range(R1)]
        scattered = [sem(f"scattered{r}") for r in range(R1)]
        consts = sem("consts")
        waits_passed = sem("waits_passed")
        wT_ready = sem("wT_ready")
        wT_done = sem("wT_done")
        wqk_ready = sem("wqk_ready")
        wqk_done = sem("wqk_done")
        wh_done = sem("wh_done")
        wl_done = sem("wl_done")
        ln1_stats = sem("ln1_stats")
        rstd1 = sem("rstd1")
        rstd2 = sem("rstd2")
        tokens_noted = sem("tokens_noted")
        ln1_norm = sem("ln1_norm")
        xT_ready = sem("xT_ready")
        xT_done = sem("xT_done")
        q_ready = sem("q_ready")
        q_done = sem("q_done")
        s_ready = sem("s_ready")
        zero_found = sem("zero_found")
        s_masked = sem("s_masked")
        p_done = sem("p_done")
        pT_ready = sem("pT_ready")
        pT_done = sem("pT_done")
        z_ready = sem("z_ready")
        z_done = sem("z_done")
        vt_ready = sem("vt_ready")
        vt_done = sem("vt_done")
        o_ready = sem("o_ready")
        resid_step = sem("resid_step")
        x1_step = sem("x1_step")
        ln2_norm = sem("ln2_norm")
        x2T_ready = sem("x2T_ready")
        x2T_done = sem("x2T_done")
        log_ready = sem("log_ready")
        exp_done = sem("exp_done")
        route = sem("route")
        counted = sem("counted")
        pos_ready = sem("pos_ready")
        place_step = sem("place_step")
        end_ready = sem("end_ready")
        table = sem("table")
        padded = sem("padded")
        numbered = sem("numbered")
        rows_in = [sem(f"rows_in{r}") for r in range(R2)]
        yn_done = sem("yn_done")
        yT_ready = sem("yT_ready")
        yh_done = sem("yh_done")
        yl_done = sem("yl_done")
        g_ready = sem("g_ready")
        u_ready = sem("u_ready")
        silu_done = sem("silu_done")
        h_done = sem("h_done")
        hT_ready = sem("hT_ready")
        hh_done = sem("hh_done")
        hl_done = sem("hl_done")
        y_ready = sem("y_ready")
        out_done = sem("out_done")
        out_sent = [sem(f"out_sent{r}") for r in range(R2)]

        N_CONST = 9
        LN1, RES, X1, LN2, ROUTE, COUNT, RSTD_STEPS = 4, 3, 14, 4, 15, 3, 3
        TABLE = 12

        x_v = x_d.rearrange("b (i p) d -> b p i d", p=P)

        block = ctx.enter_context(nc.Block())

        def end_waits(eng):
            eng.sem_inc(waits_passed, 1)

        def attention_steps(eng, step):
            for k in STEPS[0]:
                step(Turn(R1, 0, k))
            with eng.Fori(*STEPS[1]) as trip:
                for r in range(R1):
                    step(Turn(R1, trip, r))
            for k in STEPS[2]:
                step(Turn(R1, 0, k))

        def live(k, late):
            return not isinstance(k.trip, int) or 0 <= k.off - late < B

        def expert_steps(eng, step):
            for s in range(-1, R2 + 2):
                step(Turn(R2, 0, s))
            with eng.Fori(1, 8) as trip:
                for r in range(R2):
                    step(Turn(R2, trip, 2 + r))
            for s in range(SLOTS - 1, SLOTS + 2):
                step(Turn(R2, 0, s))

        def slot_live(s, late):
            return not isinstance(s.trip, int) or 0 <= s.off - late < SLOTS

        @block.sync
        def _(sp):
            def load_x(n):
                if n.has(R1):
                    sp.wait_ge(ln1_norm, (n - R1).count(LN1, LN1))
                sp.dma_start(xin[n.buf][:, :, :], x_v[bass.ds(n.number, 1), :, :, :].rearrange("b p i d -> (b p) i d")
                             if not isinstance(n.trip, int) else x_v[n.off]).then_inc(x_in[n.buf], 16)

            def load_res(n):
                if n.has(R1):
                    sp.wait_ge(resid_step, (n - R1).count(RES, RES))
                sp.dma_start(xres[n.buf][:, :, :], x_v[bass.ds(n.number, 1), :, :, :].rearrange("b p i d -> (b p) i d")
                             if not isinstance(n.trip, int) else x_v[n.off]).then_inc(res_in[n.buf], 16)

            load_x(Turn(R1, 0, 0))
            load_x(Turn(R1, 0, 1))
            load_res(Turn(R1, 0, 0))
            load_x(Turn(R1, 0, 2))
            for g in range(G):
                for v, src in enumerate((gate_d, up_d)):
                    sp.dma_start(wgu[:, g, v * EF:(v + 1) * EF].rearrange("p (e f) -> p e f", f=F),
                                 src[g * EPG:(g + 1) * EPG].rearrange("e p f -> p e f")).then_inc(e_in, 16)
            sp.dma_start(wd[:, :, :].rearrange("p g (c d) -> p (g c) d", d=D),
                         down_d.rearrange("e (c p) d -> p (e c) d", p=P)).then_inc(e_in, 16)
            load_x(Turn(R1, 0, 3))
            load_res(Turn(R1, 0, 1))
            load_res(Turn(R1, 0, 2))
            with sp.Fori(1, 5) as trip:
                for r in range(R1):
                    load_res(Turn(R1, trip, r))
                    load_x(Turn(R1, trip, r + 1))
            load_res(Turn(R1, 0, B - 1))

            def load_rows(s):
                if s.has(R2):
                    sp.wait_ge(out_sent[s.buf], (s - R2).round * 16 + 16)
                at = sp.value_load(slot_row[0:1, bass.ds(s.number, 1)], min_val=0, max_val=ROWS - P)
                sp.dma_start(rowin[s.buf][:, :], scratch[bass.ds(at, P), :]).then_inc(rows_in[s.buf], 16)

            sp.wait_ge(table, TABLE)
            sp.wait_ge(padded, 16 * G)
            sp.wait_ge(pad_out, 16)
            for r in range(R1):
                sp.wait_ge(scattered[r], 16 * NT * ((B - 1 - r) // R1 + 1))
            for r in range(R2):
                load_rows(Turn(R2, 0, r))
            with sp.Fori(1, 8) as trip:
                for r in range(R2):
                    load_rows(Turn(R2, trip, r))
            for s in range(8 * R2, SLOTS):
                load_rows(Turn(R2, 0, s))

        @block.gpsimd
        def _(pool):
            for t in (ident, identb):
                nc.gpsimd.memset(t[:, :], 0.0).then_inc(consts, 1)
            pool.wait_ge(consts, 2)
            for t in (ident, identb):
                nc.gpsimd.affine_select(out=t[:, :], in_=t[:, :], compare_op=ALU.not_equal, fill=1.0, base=0,
                                        pattern=[[-1, P]], channel_multiplier=1).then_inc(consts, 1)
            nc.gpsimd.memset(trineg[:, :], 0.0).then_inc(consts, 1)
            nc.gpsimd.memset(before[:, :], 0.0).then_inc(consts, 1)
            pool.wait_ge(consts, 6)
            nc.gpsimd.affine_select(out=trineg[:, :], in_=trineg[:, :], compare_op=ALU.is_ge, fill=MASKED, base=0,
                                    pattern=[[1, P]], channel_multiplier=-1).then_inc(consts, 1)
            nc.gpsimd.affine_select(out=before[:, :], in_=before[:, :], compare_op=ALU.is_ge, fill=1.0, base=0,
                                    pattern=[[-1, P]], channel_multiplier=1).then_inc(consts, 1)
            nc.gpsimd.memset(ones[:, :], 1.0)
            nc.gpsimd.memset(halfneg[:, :], -0.5)
            for g in range(G):
                nc.gpsimd.memset(prefer[:, :, g], float(G - g))
                nc.gpsimd.memset(carry[0][:, g:g + 1], float(g * REGION // P))
            nc.gpsimd.iota(partno[:, :], pattern=[[0, G]], base=0, channel_multiplier=1,
                           allow_small_or_imprecise_dtypes=True)
            nc.gpsimd.memset(padrow[:, :], 0.0)
            for r in range(R1):
                nc.gpsimd.memset(row[r][:, :, RW - 4:RW], 0.0)
            nc.gpsimd.iota(tileat[:, :, :], pattern=[[REGION, G], [P, T // P]], base=0, channel_multiplier=0,
                           allow_small_or_imprecise_dtypes=True)
            nc.gpsimd.iota(slotno[:, :, :], pattern=[[0, G], [1, SLOTS]], base=0, channel_multiplier=0,
                           allow_small_or_imprecise_dtypes=True).then_inc(consts, 1)
            pool.wait_ge(consts, N_CONST)
            for r in range(R1):
                nc.gpsimd.iota(row[r][:, :, TOKEN].bitcast(I32), pattern=[[P, NT]], base=(r - R1) * S,
                               channel_multiplier=1)
            nc.gpsimd.iota(padrow[:, TOKEN:TOKEN + 1].bitcast(I32), pattern=[[0, 1]], base=T,
                           channel_multiplier=0).then_inc(numbered, 1)
            pool.wait_ge(numbered, 1)
            for g in range(G - 1):
                pool.dma_start(scratch[G * REGION + g * P:G * REGION + (g + 1) * P, :], padrow[:, :]).then_inc(pad_out, 16)

            def deviations1(n):
                pool.wait_ge(ln1_stats, n.count(2 * NT, 2 * NT))
                if n.has(1):
                    pool.wait_ge(rstd1, n.count(RSTD_STEPS, 0))
                end_waits(pool)
                nc.gpsimd.tensor_scalar(vareps1[:, :], meanvar1[:, :, 1], LN_EPS, None, ALU.add).then_inc(rstd1, 1)
                nc.gpsimd.tensor_scalar(norm1s[n.buf][:, :, 0], meanvar1[:, :, 0], -1.0, None, ALU.mult).then_inc(rstd1, 1)
                pool.wait_ge(rstd1, n.count(RSTD_STEPS, 1))
                nc.gpsimd.tensor_tensor(norm1s[n.buf][:, :, 1], vareps1[:, :], halfneg[:, :], ALU.pow).then_inc(rstd1, 1)

            def deviations2(n):
                pool.wait_ge(x1_step, n.count(X1, X1))
                if n.has(1):
                    pool.wait_ge(rstd2, n.count(RSTD_STEPS, 0))
                end_waits(pool)
                nc.gpsimd.tensor_scalar(vareps2[:, :], meanvar2[:, :, 1], LN_EPS, None, ALU.add).then_inc(rstd2, 1)
                nc.gpsimd.tensor_scalar(row[n.buf][:, :, NEGMEAN], meanvar2[:, :, 0], -1.0, None, ALU.mult).then_inc(rstd2, 1)
                pool.wait_ge(rstd2, n.count(RSTD_STEPS, 1))
                nc.gpsimd.tensor_tensor(row[n.buf][:, :, RSTD], vareps2[:, :], halfneg[:, :], ALU.pow).then_inc(rstd2, 1)

            def scatter(n):
                pool.wait_ge(place_step, n.count(2, 2))
                pool.wait_ge(route, n.count(ROUTE, ROUTE))
                pool.wait_ge(tokens_noted, n.count(1, 1))
                pool.wait_ge(rstd2, n.count(RSTD_STEPS, RSTD_STEPS))
                end_waits(pool)
                for i in range(NT):
                    nc.gpsimd.indirect_dma_start(
                        out=scratch, out_offset=bass.IndirectOffsetOnAxis(ap=place[n.buf][:, i:i + 1], axis=0),
                        in_=row[n.buf][:, i, :], in_offset=None).then_inc(scattered[n.buf], 16)

            def residual(n):
                pool.wait_ge(s_masked, n.count(NT, NT))
                end_waits(pool)
                nc.gpsimd.tensor_scalar(u512[n.buf][:, :], negmax[n.buf][:, :], ALL_MASKED, 1.0 / S, ALU.is_gt,
                                        ALU.mult).then_inc(resid_step, 1)
                pool.wait_ge(vt_done, n.count(1, 1))
                pool.wait_ge(resid_step, n.count(RES, 1))
                if n.has(R1):
                    pool.wait_ge(x1_step, (n - R1).count(X1, X1))
                nc.gpsimd.tensor_tensor(resid[n.buf][:, :, :], vtot[n.buf][:, None, :].to_broadcast([P, NT, D]),
                                        u512[n.buf][:, :, None].to_broadcast([P, NT, D]), ALU.mult).then_inc(resid_step, 1)
                pool.wait_ge(res_in[n.buf], n.round * 16 + 16)
                pool.wait_ge(resid_step, n.count(RES, 2))
                nc.gpsimd.tensor_tensor(resid[n.buf][:, :, :], resid[n.buf][:, :, :], xres[n.buf][:, :, :],
                                        ALU.add).then_inc(resid_step, 1)

            def count(n):
                pool.wait_ge(route, n.count(ROUTE, 7))
                pk = pick[n.buf]
                nc.gpsimd.tensor_tensor(pairs[:, :, :], pk[:, 0:2, :], pk[:, 2:4, :], ALU.add).then_inc(counted, 1)
                pool.wait_ge(counted, n.count(COUNT, 1))
                nc.gpsimd.tensor_tensor(four[:, :], pairs[:, 0, :], pairs[:, 1, :], ALU.add).then_inc(counted, 1)
                pool.wait_ge(counted, n.count(COUNT, 2))
                nc.gpsimd.tensor_tensor(carry[(n + 1).buf][:, :], carry[n.buf][:, :], four[:, :], ALU.add).then_inc(counted, 1)

            def token_numbers(n):
                if n.has(R1):
                    pool.wait_ge(scattered[n.buf], (n - R1).round * 16 * NT + 16 * NT)
                end_waits(pool)
                ids = row[n.buf][:, :, TOKEN].bitcast(I32)
                nc.gpsimd.tensor_scalar(ids, ids, float(R1 * S), None, ALU.add).then_inc(tokens_noted, 1)

            def step(k):
                if live(k, 3):
                    deviations2(k - 3)
                if live(k, 2):
                    residual(k - 2)
                if live(k, -1):
                    deviations1(k + 1)
                if live(k, 4):
                    scatter(k - 4)
                if live(k, 2):
                    token_numbers(k - 2)
                if live(k, 3):
                    count(k - 3)

            attention_steps(pool, step)

            pool.wait_ge(table, 2)
            for g in range(G):
                nc.gpsimd.indirect_dma_start(
                    out=scratch, out_offset=bass.IndirectOffsetOnAxis(ap=padat[:, g:g + 1], axis=0),
                    in_=padrow[:, :], in_offset=None).then_inc(padded, 16)

            def normalise(s):
                pool.wait_ge(rows_in[s.buf], s.round * 16 + 16)
                if s.has(R2):
                    pool.wait_ge(yT_ready, (s - R2).count(1, 1))
                end_waits(pool)
                rt = rowin[s.buf]
                nc.gpsimd.tensor_scalar(yn[s.buf][:, :], rt[:, 0:D], rt[:, NEGMEAN:NEGMEAN + 1], rt[:, RSTD:RSTD + 1],
                                        ALU.add, ALU.mult).then_inc(yn_done, 1)

            def send(s):
                pool.wait_ge(out_done, s.count(1, 1))
                end_waits(pool)
                nc.gpsimd.indirect_dma_start(
                    out=out_d.rearrange("b s d -> (b s) d"),
                    out_offset=bass.IndirectOffsetOnAxis(ap=rowin[s.buf][:, TOKEN:TOKEN + 1].bitcast(I32), axis=0),
                    in_=outb[s.buf][:, :], in_offset=None, bounds_check=T - 1, oob_is_err=False
                ).then_inc(out_sent[s.buf], 16)

            AHEAD = R2 // 2
            for s in range(AHEAD):
                normalise(Turn(R2, 0, s))
            for s in range(AHEAD):
                normalise(Turn(R2, 0, s + AHEAD))
                send(Turn(R2, 0, s))
            with pool.Fori(0, 7) as trip:
                for r in range(R2):
                    normalise(Turn(R2, trip, R2 + r))
                    send(Turn(R2, trip, AHEAD + r))
            for s in range(7 * R2 + AHEAD, SLOTS):
                if s + AHEAD < SLOTS:
                    normalise(Turn(R2, 0, s + AHEAD))
                send(Turn(R2, 0, s))
            for r in range(R2):
                pool.wait_ge(out_sent[r], 16 * ((SLOTS - 1 - r) // R2 + 1))

        @block.scalar
        def _(act):
            act.dma_start(wqkv[:, :], w_d).then_inc(w_in, 16)
            act.dma_start(wrout[:, 0:G], macro_d).then_inc(r_in, 16)
            act.dma_start(wrout[:, G:NL].rearrange("p (g e) -> p g e", e=EPG),
                          micro_d.rearrange("g p e -> p g e")).then_inc(r_in, 16)
            for v, dst in enumerate((wqT, wkT)):
                act.wait_ge(wT_ready, 1)
                nc.scalar.activation(dst[:, :], ps_z[:, v * D:(v + 1) * D], ACT.Copy).then_inc(wT_done, 1)
            act.wait_ge(wqk_ready, 1)
            nc.scalar.activation(wqk[:, :], ps_s[0][:, 0:D], ACT.Copy).then_inc(wqk_done, 1)

            def softmax_exp(n, i):
                act.wait_ge(s_masked, n.count(NT, i + 1))
                nc.scalar.activation(probs[n.buf][:, OFF[i]:OFF[i] + WIDTH[i]], negs[i % 2][:, 0:WIDTH[i]], ACT.Exp,
                                     bias=negmax[n.buf][:, i:i + 1], scale=-1.0,
                                     accum_out=psums[n.buf][:, i:i + 1]).then_inc(p_done, 1)

            def copy_probsT(n, m):
                act.wait_ge(pT_ready, n.count(NT, m + 1))
                w = S - m * P
                nc.scalar.activation(probsT[m][:, 0:w], ps_pt[m % 2][:, 0:w], ACT.Copy).then_inc(pT_done, 1)

            def copy_x2T(n):
                act.wait_ge(x2T_ready, n.count(1, 1))
                nc.scalar.activation(x2T[:, :], ps_tr[:, :], ACT.Copy).then_inc(x2T_done, 1)

            def exp_logits(n):
                act.wait_ge(log_ready, n.count(1, 1))
                if n.has(1):
                    act.wait_ge(route, (n - 1).count(ROUTE, 1))
                nc.scalar.activation(elog[:, :, :], ps_log, ACT.Exp, scale=-1.0).then_inc(exp_done, 1)

            def copy_zT(n):
                act.wait_ge(z_ready, n.count(1, 1))
                nc.scalar.activation(zT[:, :], ps_z[:, :], ACT.Copy).then_inc(z_done, 1)

            def copy_xT(n):
                act.wait_ge(xT_ready, n.count(1, 1))
                nc.scalar.activation(xnT[n.buf][:, :], ps_tr[:, :], ACT.Copy,
                                     accum_out=xsum[n.buf][:, :]).then_inc(xT_done, 1)

            def copy_vtot(n):
                act.wait_ge(vt_ready, n.count(1, 1))
                if n.has(R1):
                    act.wait_ge(resid_step, (n - R1).count(RES, RES))
                nc.scalar.activation(vtot[n.buf][:, :], ps_vtot, ACT.Copy).then_inc(vt_done, 1)

            def copy_q(n):
                act.wait_ge(q_ready, n.count(1, 1))
                nc.scalar.activation(qT[n.buf][:, :], ps_o[:, :], ACT.Copy).then_inc(q_done, 1)

            def step(k):
                if live(k, 2):
                    copy_probsT(k - 2, 0)
                    copy_probsT(k - 2, 1)
                    copy_probsT(k - 2, 2)
                if live(k, 1):
                    softmax_exp(k - 1, 0)
                if live(k, 2):
                    copy_probsT(k - 2, 3)
                if live(k, 3):
                    copy_x2T(k - 3)
                if live(k, 2):
                    copy_zT(k - 2)
                if live(k, 1):
                    softmax_exp(k - 1, 1)
                    softmax_exp(k - 1, 2)
                if live(k, 3):
                    exp_logits(k - 3)
                if live(k, 0):
                    copy_xT(k)
                if live(k, 1):
                    softmax_exp(k - 1, 3)
                    copy_vtot(k - 1)
                if live(k, 0):
                    copy_q(k)

            attention_steps(act, step)

            act.wait_ge(e_in, 16 * (2 * G + 1))
            for g in range(G):
                nc.scalar.activation(wguh[:, g, :], wgu[:, g, :], ACT.Copy).then_inc(wh_done, 1)
                nc.scalar.activation(wdh[:, g, :], wd[:, g, :], ACT.Copy).then_inc(wh_done, 1)

            def step2(s):
                if slot_live(s, -1):
                    n = s + 1
                    act.wait_ge(yT_ready, n.count(1, 1))
                    if n.has(2):
                        act.wait_ge(u_ready, (n - 2).count(1, 1))
                    nc.scalar.activation(yh[n.buf % 2][:, :], ps_y[:, 0:P], ACT.Copy).then_inc(yh_done, 1)
                if slot_live(s, 0):
                    act.wait_ge(g_ready, s.count(1, 1))
                    if s.has(2):
                        act.wait_ge(h_done, (s - 2).count(EPG, EPG))
                    nc.scalar.activation(act_g[s.buf % 2][:, :], ps_g[s.buf % 2][:, :], ACT.Silu).then_inc(silu_done, 1)
                if slot_live(s, 1):
                    n = s - 1
                    act.wait_ge(hT_ready, n.count(1, 1))
                    if n.has(2):
                        act.wait_ge(y_ready, (n - 2).count(1, 1))
                    nc.scalar.activation(hh[n.buf % 2][:, :], ps_ht[:, :], ACT.Copy).then_inc(hh_done, 1)

            expert_steps(act, step2)

        @block.vector
        def _(dve):
            def place_rows(n):
                dve.wait_ge(pos_ready, n.count(1, 1))
                nc.vector.tensor_tensor(posm[:, :, :], ps_pos, pick[n.buf][:, :, :], ALU.mult).then_inc(place_step, 1)
                yield
                dve.wait_ge(place_step, n.count(2, 1))
                with nc.allow_low_precision(reason="whole numbers below 2**24, summed in float32"):
                    nc.vector.tensor_reduce(out=place[n.buf][:, :], in_=posm[:, :, :], op=ALU.add,
                                            axis=AX.X).then_inc(place_step, 1)
                yield

            def mask_scores(n, i):
                dve.wait_ge(s_ready, n.count(NT, i + 1))
                w = WIDTH[i]
                nc.vector.tensor_scalar(zmask[i % 2][:, 0:w], ps_s[i % 2][:, 0:w], 0.0, MASKED, ALU.is_equal,
                                        ALU.mult).then_inc(zero_found, 1)
                yield
                dve.wait_ge(zero_found, n.count(NT, i + 1))
                if n.has(1) or i >= 2:
                    dve.wait_ge(p_done, n.count(NT, i - 1))
                end_waits(dve)
                nc.vector.tensor_tensor_reduce(out=negs[i % 2][:, 0:w], in0=ps_s[i % 2][:, 0:w],
                                               in1=zmask[i % 2][:, 0:w], scale=-SCALE, scalar=3.0e38,
                                               op0=ALU.add, op1=ALU.min,
                                               accum_out=negmax[n.buf][:, i:i + 1]).then_inc(s_masked, 1)
                yield

            def stats1(n):
                dve.wait_ge(x_in[n.buf], n.round * 16 + 16)
                if n.has(1):
                    dve.wait_ge(ln1_stats, n.count(2 * NT, 0))
                for i in range(NT):
                    nc.vector.bn_stats(st1[:, i, :], xin[n.buf][:, i, :]).then_inc(ln1_stats, 1)
                    yield
                dve.wait_ge(ln1_stats, n.count(2 * NT, NT))
                if n.has(1):
                    dve.wait_ge(rstd1, (n - 1).count(RSTD_STEPS, 2))
                end_waits(dve)
                for i in range(NT):
                    nc.vector.bn_aggr(meanvar1[:, i, :], st1[:, i, :]).then_inc(ln1_stats, 1)
                    yield

            def norm1(n):
                dve.wait_ge(rstd1, n.count(RSTD_STEPS, RSTD_STEPS))
                if n.has(R1):
                    dve.wait_ge(z_ready, (n - R1).count(1, 1))
                for i in range(NT):
                    nc.vector.tensor_scalar(xn[n.buf][:, i, :], xin[n.buf][:, i, :], norm1s[n.buf][:, i, 0:1],
                                            norm1s[n.buf][:, i, 1:2], ALU.add, ALU.mult).then_inc(ln1_norm, 1)
                    yield

            def norm2(n):
                dve.wait_ge(rstd2, n.count(RSTD_STEPS, RSTD_STEPS))
                if n.has(R1):
                    dve.wait_ge(x2T_ready, (n - R1).count(1, 1))
                for i in range(NT):
                    nc.vector.tensor_scalar(xn2[n.buf][:, i, :], row[n.buf][:, i, 0:D], row[n.buf][:, i, NEGMEAN:NEGMEAN + 1],
                                            row[n.buf][:, i, RSTD:RSTD + 1], ALU.add, ALU.mult).then_inc(ln2_norm, 1)
                    yield

            def new_x(n):
                dve.wait_ge(p_done, n.count(NT, NT))
                nc.vector.reciprocal(rsum[:, :], psums[n.buf][:, :]).then_inc(x1_step, 1)
                yield
                dve.wait_ge(x1_step, n.count(X1, 1))
                nc.vector.scalar_tensor_tensor(out=rlive[:, :], in0=negmax[n.buf][:, :], scalar=ALL_MASKED,
                                               in1=rsum[:, :], op0=ALU.is_le, op1=ALU.mult).then_inc(x1_step, 1)
                yield
                dve.wait_ge(x1_step, n.count(X1, 2))
                dve.wait_ge(resid_step, n.count(RES, RES))
                if n.has(R1):
                    dve.wait_ge(scattered[n.buf], (n - R1).round * 16 * NT + 16 * NT)
                dve.wait_ge(o_ready, n.count(1, 1))
                for i in range(NT):
                    nc.vector.scalar_tensor_tensor(out=row[n.buf][:, i, 0:D], in0=ps_o[:, i * D:(i + 1) * D],
                                                   scalar=rlive[:, i:i + 1], in1=resid[n.buf][:, i, :],
                                                   op0=ALU.mult, op1=ALU.add).then_inc(x1_step, 1)
                    yield
                dve.wait_ge(x1_step, n.count(X1, 2 + NT))
                for i in range(NT):
                    nc.vector.bn_stats(st2[:, i, :], row[n.buf][:, i, 0:D]).then_inc(x1_step, 1)
                    yield
                dve.wait_ge(x1_step, n.count(X1, 2 + 2 * NT))
                if n.has(1):
                    dve.wait_ge(rstd2, (n - 1).count(RSTD_STEPS, 2))
                end_waits(dve)
                for i in range(NT):
                    nc.vector.bn_aggr(meanvar2[:, i, :], st2[:, i, :]).then_inc(x1_step, 1)
                    yield

            def routed(n, done):
                dve.wait_ge(route, n.count(ROUTE, done))

            def pick_group(n):
                def after(done):
                    routed(n, done)

                dve.wait_ge(exp_done, n.count(1, 1))
                nc.vector.tensor_scalar(elog1[:, :, :], elog[:, :, :], 1.0, None, ALU.add).then_inc(route, 1)
                yield
                after(1)
                nc.vector.reciprocal(sig[:, :, :], elog1[:, :, :]).then_inc(route, 1)
                yield
                after(2)
                nc.vector.tensor_reduce(out=top[:, :], in_=sig[:, :, 0:G], op=ALU.max, axis=AX.X).then_inc(route, 1)
                yield
                after(3)
                nc.vector.tensor_tensor(istop[:, :, :], sig[:, :, 0:G], top[:, :, None].to_broadcast([P, NT, G]),
                                        ALU.is_equal).then_inc(route, 1)
                yield
                after(4)
                nc.vector.tensor_tensor(rank[:, :, :], istop[:, :, :], prefer[:, :, :], ALU.mult).then_inc(route, 1)
                yield
                after(5)
                nc.vector.tensor_reduce(out=toprank[:, :], in_=rank[:, :, :], op=ALU.max, axis=AX.X).then_inc(route, 1)
                yield
                after(6)
                nc.vector.tensor_tensor(pick[n.buf][:, :, :], rank[:, :, :],
                                        toprank[:, :, None].to_broadcast([P, NT, G]), ALU.is_equal).then_inc(route, 1)
                yield

            def pick_experts(n):
                def after(done):
                    routed(n, done)

                after(7)
                nc.vector.tensor_tensor(micro[:, :, :, :], sig[:, :, G:NL].rearrange("p i (g e) -> p i g e", e=EPG),
                                        pick[n.buf][:, :, :, None].to_broadcast([P, NT, G, EPG]),
                                        ALU.mult).then_inc(route, 1)
                nc.vector.tensor_scalar(tope[:, :], top[:, :], TOP_EPS, None, ALU.add).then_inc(route, 1)
                yield
                after(9)
                nc.vector.tensor_reduce(out=msel[:, :, :], in_=micro[:, :, :, :].rearrange("p i g e -> p i e g"),
                                        op=ALU.add, axis=AX.X).then_inc(route, 1)
                yield
                after(10)
                nc.vector.tensor_tensor(msum[:, :], msel[:, :, 0], msel[:, :, 1], ALU.add).then_inc(route, 1)
                yield
                after(11)
                nc.vector.scalar_tensor_tensor(out=wden[:, :], in0=msum[:, :], scalar=TOP_EPS, in1=tope[:, :],
                                               op0=ALU.add, op1=ALU.mult).then_inc(route, 1)
                yield
                after(12)
                nc.vector.reciprocal(wrec[:, :], wden[:, :]).then_inc(route, 1)
                yield
                after(13)
                nc.vector.tensor_tensor(wtop[:, :], wrec[:, :], top[:, :], ALU.mult).then_inc(route, 1)
                yield
                after(14)
                nc.vector.tensor_tensor(row[n.buf][:, :, WGT:WGT + EPG], msel[:, :, :],
                                        wtop[:, :, None].to_broadcast([P, NT, EPG]), ALU.mult).then_inc(route, 1)
                yield

            ORDER = "s w s w s w s w 0 w p w 0 w p m m m m s s s s 1 n n 1 n n 2 x x 2 x x x x 3 r x r x 3 r x r x x x r x x r r"

            def step(k):
                kinds = {"p": (4, lambda: place_rows(k - 4)), "n": (0, lambda: norm1(k)), "m": (3, lambda: norm2(k - 3)),
                         "s": (-1, lambda: stats1(k + 1)), "r": (3, lambda: pick_group(k - 3)), "w": (4, lambda: pick_experts(k - 4)), "x": (2, lambda: new_x(k - 2))}
                for i in range(NT):
                    kinds[str(i)] = (1, lambda i=i: mask_scores(k - 1, i))
                going = {c: make() for c, (late, make) in kinds.items() if live(k, late)}
                for c in ORDER.split():
                    if c in going:
                        next(going[c], None)

            dve.wait_ge(consts, N_CONST)
            attention_steps(dve, step)

            def after(done):
                dve.wait_ge(table, done)

            dve.wait_ge(end_ready, 1)
            nc.vector.tensor_copy(ends[:, :], ps_end).then_inc(table, 1)
            after(1)
            nc.vector.tensor_tensor(padat[:, :], ends[:, :], partno[:, :], ALU.add).then_inc(table, 1)
            nc.vector.tensor_tensor(tilehit[:, :, :], tileat[:, :, :], ends[0:1, :, None].to_broadcast([1, G, T // P]),
                                    ALU.is_lt).then_inc(table, 1)
            after(3)
            nc.vector.tensor_reduce(out=tiles[:, :], in_=tilehit[:, :, :], op=ALU.add, axis=AX.X).then_inc(table, 1)
            after(4)
            nc.vector.tensor_scalar(skip[:, :], tiles[:, :], -float(P), float(REGION), ALU.mult, ALU.add).then_inc(table, 1)
            nc.vector.tensor_tensor_scan(out=tcum[:, :], data0=ones[0:1, 0:G], data1=tiles[:, :], initial=0.0,
                                         op0=ALU.mult, op1=ALU.add).then_inc(table, 1)
            after(6)
            nc.vector.tensor_tensor(past[:, :, :], slotno[:, :, :], tcum[:, :, None].to_broadcast([1, G, SLOTS]),
                                    ALU.is_ge).then_inc(table, 1)
            after(7)
            nc.vector.tensor_tensor(pastskip[:, :, :], past[:, :, :], skip[:, :, None].to_broadcast([1, G, SLOTS]),
                                    ALU.mult).then_inc(table, 1)
            nc.vector.tensor_reduce(out=grp_f[:, :], in_=past[:, :, :].rearrange("p g s -> p s g"), op=ALU.add,
                                    axis=AX.X).then_inc(table, 1)
            after(9)
            nc.vector.tensor_scalar(slot_group[:, :], grp_f[:, :], float(G - 1), None, ALU.min).then_inc(table, 1)
            nc.vector.tensor_reduce(out=rowsum[:, :], in_=pastskip[:, :, :].rearrange("p g s -> p s g"), op=ALU.add,
                                    axis=AX.X).then_inc(table, 1)
            after(11)
            nc.vector.scalar_tensor_tensor(out=slot_row[:, :], in0=slotno[:, 0, :], scalar=float(P), in1=rowsum[:, :],
                                           op0=ALU.mult, op1=ALU.add).then_inc(table, 1)

            for g in range(G):
                dve.wait_ge(wh_done, 2 * g + 1)
                nc.vector.tensor_tensor(wgul[:, g, :], wgu[:, g, :], wguh[:, g, :].bitcast(F32),
                                        ALU.subtract).then_inc(wl_done, 1)
                dve.wait_ge(wh_done, 2 * g + 2)
                nc.vector.tensor_tensor(wdl[:, g, :], wd[:, g, :], wdh[:, g, :].bitcast(F32),
                                        ALU.subtract).then_inc(wl_done, 1)

            def step2(s):
                if slot_live(s, -1):
                    n = s + 1
                    dve.wait_ge(yh_done, n.count(1, 1))
                    nc.vector.tensor_tensor(yl[n.buf % 2][:, :], ps_y[:, 0:P], yh[n.buf % 2][:, :].bitcast(F32),
                                            ALU.subtract).then_inc(yl_done, 1)
                if slot_live(s, 0):
                    dve.wait_ge(silu_done, s.count(1, 1))
                    dve.wait_ge(u_ready, s.count(1, 1))
                    if s.has(2):
                        dve.wait_ge(hT_ready, (s - 2).count(1, 1))
                    for e in range(EPG):
                        nc.vector.scalar_tensor_tensor(
                            out=hid[s.buf % 2][:, e * F:(e + 1) * F], in0=act_g[s.buf % 2][:, e * F:(e + 1) * F],
                            scalar=rowin[s.buf][:, WGT + e:WGT + e + 1], in1=ps_u[s.buf % 2][:, e * F:(e + 1) * F],
                            op0=ALU.mult, op1=ALU.mult).then_inc(h_done, 1)
                if slot_live(s, 1):
                    n = s - 1
                    dve.wait_ge(hh_done, n.count(1, 1))
                    nc.vector.tensor_tensor(hl[n.buf % 2][:, :], ps_ht[:, :], hh[n.buf % 2][:, :].bitcast(F32),
                                            ALU.subtract).then_inc(hl_done, 1)
                if slot_live(s, 2):
                    n = s - 2
                    dve.wait_ge(y_ready, n.count(1, 1))
                    if n.has(R2):
                        dve.wait_ge(out_sent[n.buf], (n - R2).round * 16 + 16)
                    nc.vector.tensor_tensor(outb[n.buf][:, :], ps_out[:, 0:D], rowin[n.buf][:, 0:D],
                                            ALU.add).then_inc(out_done, 1)

            expert_steps(dve, step2)

        @block.tensor
        def _(pe):
            pe.wait_ge(w_in, 16)
            pe.wait_ge(consts, N_CONST)
            nc.tensor.transpose(ps_z[:, 0:D], wqkv[:, 0:D], ident[:, :])
            nc.tensor.transpose(ps_z[:, D:2 * D], wqkv[:, D:2 * D], ident[:, :]).then_inc(wT_ready, 1)
            pe.wait_ge(wT_done, 2)
            nc.tensor.matmul(ps_s[0][:, 0:D], wqT[:, :], wkT[:, :], start=True, stop=True).then_inc(wqk_ready, 1)
            pe.wait_ge(wqk_done, 1)
            pe.wait_ge(r_in, 32)

            def positions(n):
                pe.wait_ge(route, n.count(ROUTE, 7))
                if n.has(1):
                    pe.wait_ge(counted, (n - 1).count(COUNT, COUNT))
                if live(n, -2):
                    pe.wait_ge(vt_done, (n + 2).count(1, 1))
                pk = pick[n.buf]
                nc.tensor.matmul(ps_pos, before[:, :], pk[:, :, :], start=True, stop=False)
                nc.tensor.matmul(ps_pos, ones[:, :], carry[n.buf][:, None, :].to_broadcast([P, NT, G]),
                                 start=False, stop=False)
                for i in range(NT - 1):
                    last = nc.tensor.matmul(ps_pos[:, i + 1:NT, :], ones[:, :],
                                            pk[:, i:i + 1, :].to_broadcast([P, NT - 1 - i, G]),
                                            start=False, stop=i == NT - 2)
                last.then_inc(pos_ready, 1)

            def scores(n, i):
                pe.wait_ge(q_done, n.count(1, 1))
                if n.has(1) or i >= 2:
                    pe.wait_ge(s_masked, n.count(NT, i - 1))
                nc.tensor.matmul(ps_s[i % 2][:, 0:WIDTH[i]], qT[n.buf][:, i * P:(i + 1) * P],
                                 xnT[n.buf][:, i * P:S], start=True, stop=False)
                nc.tensor.matmul(ps_s[i % 2][:, 0:P], identb[:, :], trineg[:, :],
                                 start=False, stop=True).then_inc(s_ready, 1)

            def transpose_probs(n, m):
                pe.wait_ge(p_done, n.count(NT, NT))
                if n.has(1) or m >= 2:
                    pe.wait_ge(pT_done, n.count(NT, m - 1))
                j = NT - 1 - m
                for i in range(j + 1):
                    at = OFF[i] + (j - i) * P
                    last = nc.tensor.transpose(ps_pt[m % 2][:, i * P:(i + 1) * P], probs[n.buf][:, at:at + P], ident[:, :])
                last.then_inc(pT_ready, 1)

            def weigh(n, m):
                pe.wait_ge(pT_done, n.count(NT, m + 1))
                if m == 0 and n.has(1):
                    pe.wait_ge(z_done, n.count(1, 0))
                j = NT - 1 - m
                mm = nc.tensor.matmul(ps_z[:, 0:(j + 1) * P], xn[n.buf][:, j, :], probsT[m][:, 0:(j + 1) * P],
                                      start=m == 0, stop=m == NT - 1)
                if m == NT - 1:
                    mm.then_inc(z_ready, 1)

            def transpose_x2(n):
                pe.wait_ge(ln2_norm, n.count(LN2, LN2))
                if live(n, -2):
                    pe.wait_ge(xT_done, (n + 2).count(1, 1))
                elif n.has(1):
                    pe.wait_ge(x2T_done, n.count(1, 0))
                for i in range(NT):
                    last = nc.tensor.transpose(ps_tr[:, i * P:(i + 1) * P], xn2[n.buf][:, i, :], ident[:, :])
                last.then_inc(x2T_ready, 1)

            def logits(n):
                pe.wait_ge(x2T_done, n.count(1, 1))
                if n.has(1):
                    pe.wait_ge(place_step, (n - 1).count(2, 1))
                else:
                    pe.wait_ge(vt_done, (n + 1).count(1, 1))
                for i in range(NT):
                    last = nc.tensor.matmul(ps_log[:, i, :], x2T[:, i * P:(i + 1) * P], wrout[:, :],
                                            start=True, stop=True)
                last.then_inc(log_ready, 1)

            def transpose_x(n):
                pe.wait_ge(ln1_norm, n.count(LN1, LN1))
                if n.has(3):
                    pe.wait_ge(x2T_done, (n - 3).count(1, 1))
                elif n.has(1):
                    pe.wait_ge(xT_done, n.count(1, 0))
                for i in range(NT):
                    last = nc.tensor.transpose(ps_tr[:, i * P:(i + 1) * P], xn[n.buf][:, i, :], ident[:, :])
                last.then_inc(xT_ready, 1)

            def queries(n):
                pe.wait_ge(xT_done, n.count(1, 1))
                if n.has(2):
                    pe.wait_ge(x1_step, (n - 2).count(X1, 2 + NT))
                elif n.has(1):
                    pe.wait_ge(q_done, n.count(1, 0))
                nc.tensor.matmul(ps_o[:, :], wqk[:, :], xnT[n.buf][:, :], start=True, stop=True).then_inc(q_ready, 1)

            def value_total(n):
                if n.has(2):
                    pe.wait_ge(exp_done, (n - 2).count(1, 1))
                nc.tensor.matmul(ps_vtot, xsum[n.buf][:, 0:1].to_broadcast([P, P]), wqkv[:, 2 * D:3 * D],
                                 start=True, stop=True).then_inc(vt_ready, 1)

            def attend(n):
                pe.wait_ge(z_done, n.count(1, 1))
                if live(n, -1):
                    pe.wait_ge(q_done, (n + 1).count(1, 1))
                else:
                    pe.wait_ge(x1_step, (n - 1).count(X1, 2 + NT))
                for i in range(NT):
                    last = nc.tensor.matmul(ps_o[:, i * D:(i + 1) * D], zT[:, i * P:(i + 1) * P],
                                            wqkv[:, 2 * D:3 * D], start=True, stop=True)
                last.then_inc(o_ready, 1)

            def step(k):
                if live(k, 2):
                    transpose_probs(k - 2, 0)
                if live(k, 1):
                    scores(k - 1, 0)
                if live(k, 4):
                    positions(k - 4)
                if live(k, 2):
                    transpose_probs(k - 2, 1)
                    weigh(k - 2, 0)
                    transpose_probs(k - 2, 2)
                    transpose_probs(k - 2, 3)
                    weigh(k - 2, 1)
                if live(k, 1):
                    scores(k - 1, 1)
                if live(k, 2):
                    weigh(k - 2, 2)
                    weigh(k - 2, 3)
                if live(k, 3):
                    transpose_x2(k - 3)
                if live(k, 1):
                    scores(k - 1, 2)
                if live(k, 2):
                    attend(k - 2)
                if live(k, 3):
                    logits(k - 3)
                if live(k, 0):
                    transpose_x(k)
                if live(k, 1):
                    scores(k - 1, 3)
                    value_total(k - 1)
                if live(k, 0):
                    queries(k)

            attention_steps(pe, step)

            pe.wait_ge(counted, B * COUNT)
            pe.wait_ge(place_step, 2 * B)
            nc.tensor.matmul(ps_end, ones[:, :], carry[B % R1][:, :], start=True, stop=True).then_inc(end_ready, 1)

            pe.wait_ge(wl_done, 2 * G)
            pe.wait_ge(table, TABLE)

            def group_of(s):
                return pe.value_load(slot_group[0:1, bass.ds(s.number, 1)], min_val=0, max_val=G - 1)

            def split_matmul(out, hi, lo, whi, wlo, start, stop):
                nc.tensor.matmul(out, hi, whi, start=start, stop=False)
                nc.tensor.matmul(out, hi, wlo, start=False, stop=False)
                return nc.tensor.matmul(out, lo, whi, start=False, stop=stop)

            def step2(s):
                if slot_live(s, 0):
                    g = group_of(s)
                if slot_live(s, -1):
                    n = s + 1
                    pe.wait_ge(yn_done, n.count(1, 1))
                    if n.has(1):
                        pe.wait_ge(yl_done, n.count(1, 0))
                    nc.tensor.transpose(ps_y[:, 0:P], yn[n.buf][:, :], ident[:, :]).then_inc(yT_ready, 1)
                if slot_live(s, 0):
                    b = s.buf % 2
                    pe.wait_ge(yl_done, s.count(1, 1))
                    if s.has(2):
                        pe.wait_ge(silu_done, (s - 2).count(1, 1))
                    split_matmul(ps_g[b][:, :], yh[b][:, :], yl[b][:, :],
                                 wguh[:, bass.ds(g, 1), 0:EF].rearrange("p g f -> p (g f)"),
                                 wgul[:, bass.ds(g, 1), 0:EF].rearrange("p g f -> p (g f)"),
                                 True, True).then_inc(g_ready, 1)
                if slot_live(s, 2):
                    gd = group_of(s - 2)
                if slot_live(s, 1):
                    n = s - 1
                    pe.wait_ge(h_done, n.count(EPG, EPG))
                    if n.has(1):
                        pe.wait_ge(hl_done, n.count(1, 0))
                    for c in range(NC):
                        last = nc.tensor.transpose(ps_ht[:, c * P:(c + 1) * P], hid[n.buf % 2][:, c * P:(c + 1) * P],
                                                   ident[:, :])
                    last.then_inc(hT_ready, 1)
                if slot_live(s, 0):
                    if s.has(2):
                        pe.wait_ge(h_done, (s - 2).count(EPG, EPG))
                    split_matmul(ps_u[b][:, :], yh[b][:, :], yl[b][:, :],
                                 wguh[:, bass.ds(g, 1), EF:2 * EF].rearrange("p g f -> p (g f)"),
                                 wgul[:, bass.ds(g, 1), EF:2 * EF].rearrange("p g f -> p (g f)"),
                                 True, True).then_inc(u_ready, 1)
                if slot_live(s, 2):
                    n = s - 2
                    pe.wait_ge(hl_done, n.count(1, 1))
                    if n.has(1):
                        pe.wait_ge(out_done, n.count(1, 0))
                    for c in range(NC):
                        last = split_matmul(ps_out[:, 0:D], hh[n.buf % 2][:, c * P:(c + 1) * P],
                                            hl[n.buf % 2][:, c * P:(c + 1) * P],
                                            wdh[:, bass.ds(gd, 1), c * D:(c + 1) * D].rearrange("p g f -> p (g f)"),
                                            wdl[:, bass.ds(gd, 1), c * D:(c + 1) * D].rearrange("p g f -> p (g f)"),
                                            c == 0, c == NC - 1)
                    last.then_inc(y_ready, 1)

            expert_steps(pe, step2)


_INS = ['L0_attn_x', 'L0_attn_W', 'L0_ffn_macro_w', 'L0_ffn_micro_w', 'L0_ffn_gate_w', 'L0_ffn_up_w', 'L0_ffn_down_w']
_OUTS = [((16, 512, 128), 'float32')]


def kernel(**inputs):
    import numpy as _np
    import concourse.bacc as _bacc
    from concourse import mybir as _mybir
    from concourse.bass_utils import run_bass_kernel_spmd as _run

    nc = _bacc.Bacc("TRN2", target_bir_lowering=False, num_devices=1)
    arrays, args = {}, []
    for name in _INS:
        a = _np.ascontiguousarray(inputs[name])
        arrays[f"in_{name}_dram"] = a
        args.append(nc.dram_tensor(f"in_{name}_dram", a.shape, _mybir.dt.from_np(a.dtype), kind="ExternalInput").ap())
    for i, (shape, dtype) in enumerate(_OUTS):
        dt = _mybir.dt.from_np(_np.dtype(dtype))
        args.append(nc.dram_tensor(f"out_{i}_dram", shape, dt, kind="ExternalOutput").ap())
    preln_attention_moe_kernel(nc, *args)
    r = _run(nc, [arrays], core_ids=[0])
    got = tuple(r.results[0][f"out_{i}_dram"] for i in range(len(_OUTS)))
    return got[0]
```

```python
import concourse.bass as bass
from concourse import mybir
from contextlib import ExitStack

F32 = mybir.dt.float32
F32R = mybir.dt.float32r
BF16 = mybir.dt.bfloat16
F16 = mybir.dt.float16
I32 = mybir.dt.int32
ALU = mybir.AluOpType
ACT = mybir.ActivationFunctionType
AX = mybir.AxisListType

P = 128


class Turn:

    def __init__(self, ring, trip, off):
        self.ring, self.trip, self.off = ring, trip, off
        self.buf = off % ring
        self.number = off if isinstance(trip, int) else ring * trip + off
        self.round = off // ring if isinstance(trip, int) else trip + off // ring

    def __add__(self, d):
        return Turn(self.ring, self.trip, self.off + d)

    def __sub__(self, d):
        return self + -d

    def has(self, earlier):
        return not isinstance(self.trip, int) or self.off >= earlier

    def count(self, per, more):
        return self.number * per + more


def preln_attention_moe_kernel(nc, x_d, w_d, macro_d, micro_d, gate_d, up_d, down_d, out_d):
    B, S, D = x_d.shape
    NT = S // P
    T = B * S
    G, _, EPG = micro_d.shape
    F = gate_d.shape[2]
    EF = EPG * F
    NC = EF // P
    NL = G + G * EPG
    SCALE = 1.0 / float(D) ** 0.5
    MASKED = -2.0 ** 53
    ALL_MASKED = 1e14
    LN_EPS, TOP_EPS = 1e-5, 1e-9
    WIDTH = [S - P * i for i in range(NT)]
    OFF = [sum(WIDTH[:i]) for i in range(NT)]
    SW = sum(WIDTH)
    NEGMEAN, RSTD, WGT, TOKEN, RW = D, D + 1, D + 2, D + 4, D + 8
    REGION = T + P
    SLOTS = T // P + G - 1
    ROWS = G * REGION + (G - 1) * P
    R1 = 3
    R2 = 8
    STEPS = [list(range(-2, 6)), (2, 4), list(range(12, 20))]
    assert B == 16 and NT == 4 and R1 * 5 + 1 == B and SLOTS == 67

    scratch = nc.dram_tensor("sorted_rows", [ROWS, RW], F32).ap()

    ctx = ExitStack()
    with ctx:
        def sb(name, shape, dt=F32):
            return ctx.enter_context(nc.sbuf_tensor(name, shape, dt))

        def sem(name):
            return ctx.enter_context(nc.semaphore(name))

        ident = sb("ident", [P, P])
        identb = sb("identb", [P, P], BF16)
        trineg = sb("trineg", [P, P], BF16)
        before = sb("before", [P, P], F16)
        ones = sb("ones", [P, P], F16)
        halfneg = sb("halfneg", [P, NT])
        prefer = sb("prefer", [P, NT, G])
        padrow = sb("padrow", [P, RW])
        wqkv = sb("wqkv", [P, 3 * D])
        wqT = sb("wqT", [P, D])
        wkT = sb("wkT", [P, D])
        wqk = sb("wqk", [P, D])
        wrout = sb("wrout", [P, NL])
        wgu = sb("wgu", [P, G, 2 * EF])
        wguh = sb("wguh", [P, G, 2 * EF], F32R)
        wgul = sb("wgul", [P, G, 2 * EF], F32R)
        wd = sb("wd", [P, G, NC, D])
        wds = sb("wds", [P, G, NC, 2, D], F32R)
        xin = [sb(f"xin{r}", [P, NT, D]) for r in range(R1)]
        xres = [sb(f"xres{r}", [P, NT, D]) for r in range(R1)]
        st1 = sb("st1", [P, NT, 6])
        meanvar1 = sb("meanvar1", [P, NT, 2])
        vareps1 = sb("vareps1", [P, NT])
        negmean1 = sb("negmean1", [P, NT])
        norm1s = [sb(f"norm1s{r}", [P, NT, 2]) for r in range(R1)]
        xn = [sb(f"xn{r}", [P, NT, D]) for r in range(R1)]
        xnT = [sb(f"xnT{r}", [P, S]) for r in range(R1)]
        xsum = [sb(f"xsum{r}", [P, 1]) for r in range(R1)]
        qT = [sb(f"qT{r}", [P, S]) for r in range(R1)]
        zmask = [sb(f"zmask{r}", [P, S]) for r in range(2)]
        negs = [sb(f"negs{r}", [P, S]) for r in range(2)]
        negmax = [sb(f"negmax{r}", [P, NT]) for r in range(R1)]
        probs = [sb(f"probs{r}", [P, SW]) for r in range(R1)]
        psums = [sb(f"psums{r}", [P, NT]) for r in range(R1)]
        probsT = [sb(f"probsT{m}", [P, S]) for m in range(NT)]
        zT = sb("zT", [P, S])
        vtot = [sb(f"vtot{r}", [P, D]) for r in range(R1)]
        u512 = [sb(f"u512_{r}", [P, NT]) for r in range(R1)]
        resid = [sb(f"resid{r}", [P, NT, D]) for r in range(R1)]
        rsum = sb("rsum", [P, NT])
        rlive = sb("rlive", [P, NT])
        row = [sb(f"row{r}", [P, NT, RW]) for r in range(R1)]
        st2 = sb("st2", [P, NT, 6])
        meanvar2 = sb("meanvar2", [P, NT, 2])
        vareps2 = sb("vareps2", [P, NT])
        xn2 = [sb(f"xn2_{r}", [P, NT, D]) for r in range(R1)]
        x2T = sb("x2T", [P, S])
        elog = sb("elog", [P, NT, NL])
        elog1 = sb("elog1", [P, NT, NL])
        sig = sb("sig", [P, NT, NL])
        top = sb("top", [P, NT])
        istop = sb("istop", [P, NT, G])
        rank = sb("rank", [P, NT, G])
        toprank = sb("toprank", [P, NT])
        pick = [sb(f"pick{r}", [P, NT, G], F16) for r in range(R1)]
        micro = sb("micro", [P, NT, G, EPG])
        msel = sb("msel", [P, NT, EPG])
        msum = sb("msum", [P, NT])
        tope = sb("tope", [P, NT])
        wden = sb("wden", [P, NT])
        wrec = sb("wrec", [P, NT])
        wtop = sb("wtop", [P, NT])
        four = sb("four", [P, G], F16)
        carry = [sb(f"carry{r}", [P, G], F16) for r in range(R1)]
        posm = sb("posm", [P, NT, G])
        place = [sb(f"place{r}", [P, NT], I32) for r in range(R1)]
        ends = sb("ends", [1, G])
        padat = sb("padat", [1, G], I32)
        tileat = sb("tileat", [1, G, T // P])
        tilehit = sb("tilehit", [1, G, T // P])
        tiles = sb("tiles", [1, G])
        tcum = sb("tcum", [1, G])
        skip = sb("skip", [1, G])
        slotno = sb("slotno", [1, G, SLOTS])
        past = sb("past", [1, G, SLOTS])
        pastskip = sb("pastskip", [1, G, SLOTS])
        grp_f = sb("grp_f", [1, SLOTS])
        rowsum = sb("rowsum", [1, SLOTS])
        slot_group = sb("slot_group", [1, SLOTS], I32)
        slot_row = sb("slot_row", [1, SLOTS], I32)
        rowin = [sb(f"rowin{r}", [P, RW]) for r in range(R2)]
        yn = [sb(f"yn{r}", [P, D]) for r in range(R2)]
        yh = [sb(f"yh{r}", [P, P], F32R) for r in range(2)]
        yl = [sb(f"yl{r}", [P, P], F32R) for r in range(2)]
        silu_first = sb("silu_first", [P, 1])
        act_g = [sb(f"act_g{r}", [P, EF]) for r in range(2)]
        hid = [sb(f"hid{r}", [P, EF]) for r in range(2)]
        hh = [sb(f"hh{r}", [P, EF], F32R) for r in range(2)]
        hl = [sb(f"hl{r}", [P, EF], F32R) for r in range(2)]
        outx = sb("outx", [P, D])
        outb = [sb(f"outb{r}", [P, D]) for r in range(R2)]

        bank = [ctx.enter_context(nc.psum_tensor(f"bank{i}", [P, 512], F32)) for i in range(8)]
        ps_tr, ps_z, ps_o, ps_m = bank[0], bank[1], bank[6], bank[7]
        ps_s, ps_pt = bank[2:4], bank[4:6]
        ps_vtot = ps_m[:, 0:D]
        ps_log = ps_m[:, D:D + NT * NL].rearrange("p (i l) -> p i l", l=NL)
        ps_pos = ps_m[:, 192:192 + NT * G].rearrange("p (i g) -> p i g", g=G)
        ps_end = ps_m[:, 256:256 + G]
        ps_y, ps_g, ps_u, ps_ht, ps_out = bank[0], bank[1:3], bank[3:5], bank[5], bank[6]

        w_in = sem("w_in")
        r_in = sem("r_in")
        e_in = [sem(f"e_in{g}") for g in range(G)]
        pad_out = sem("pad_out")
        x_in = [sem(f"x_in{r}") for r in range(R1)]
        res_in = [sem(f"res_in{r}") for r in range(R1)]
        scattered = [sem(f"scattered{r}") for r in range(R1)]
        consts = sem("consts")
        waits_passed = sem("waits_passed")
        wT_ready = sem("wT_ready")
        wT_done = sem("wT_done")
        wqk_ready = sem("wqk_ready")
        wqk_done = sem("wqk_done")
        wh_done = sem("wh_done")
        wl_done = sem("wl_done")
        ln1_stats = sem("ln1_stats")
        rstd1 = sem("rstd1")
        rstd2 = sem("rstd2")
        tokens_noted = sem("tokens_noted")
        ln1_norm = sem("ln1_norm")
        xT_ready = sem("xT_ready")
        xT_done = sem("xT_done")
        q_ready = sem("q_ready")
        q_done = sem("q_done")
        s_ready = sem("s_ready")
        zero_found = sem("zero_found")
        s_masked = sem("s_masked")
        p_done = sem("p_done")
        pT_ready = sem("pT_ready")
        pT_done = sem("pT_done")
        z_ready = sem("z_ready")
        z_done = sem("z_done")
        vt_ready = sem("vt_ready")
        vt_done = sem("vt_done")
        o_ready = sem("o_ready")
        masked_found = sem("masked_found")
        resid_step = sem("resid_step")
        x1_step = sem("x1_step")
        ln2_norm = sem("ln2_norm")
        x2T_ready = sem("x2T_ready")
        x2T_done = sem("x2T_done")
        log_ready = sem("log_ready")
        exp_done = sem("exp_done")
        route = sem("route")
        counted = sem("counted")
        pos_ready = sem("pos_ready")
        place_step = sem("place_step")
        end_ready = sem("end_ready")
        table = sem("table")
        padded = sem("padded")
        numbered = sem("numbered")
        slots_numbered = sem("slots_numbered")
        rows_in = [sem(f"rows_in{r}") for r in range(R2)]
        yn_done = sem("yn_done")
        yT_ready = sem("yT_ready")
        yh_done = sem("yh_done")
        yl_done = sem("yl_done")
        g_ready = sem("g_ready")
        u_ready = sem("u_ready")
        silu_done = sem("silu_done")
        h_done = sem("h_done")
        hT_ready = sem("hT_ready")
        hh_done = sem("hh_done")
        hl_done = sem("hl_done")
        y_ready = sem("y_ready")
        out_part = sem("out_part")
        out_done = sem("out_done")
        out_sent = [sem(f"out_sent{r}") for r in range(R2)]

        N_CONST = 9
        LN1, RES, X1, LN2, ROUTE, COUNT, RSTD1, RSTD2 = 4, 2, 14, 4, 15, 2, 4, 3
        TABLE = 12

        x_v = x_d.rearrange("b (i p) d -> b p i d", p=P)

        block = ctx.enter_context(nc.Block())

        def end_waits(eng):
            eng.sem_inc(waits_passed, 1)

        def attention_steps(eng, step):
            for k in STEPS[0]:
                step(Turn(R1, 0, k))
            with eng.Fori(*STEPS[1]) as trip:
                for r in range(R1):
                    step(Turn(R1, trip, r))
            for k in STEPS[2]:
                step(Turn(R1, 0, k))

        def live(k, late):
            return not isinstance(k.trip, int) or 0 <= k.off - late < B

        def expert_steps(eng, step):
            for s in range(-1, R2 + 2):
                step(Turn(R2, 0, s))
            with eng.Fori(1, 8) as trip:
                for r in range(R2):
                    step(Turn(R2, trip, 2 + r))
            for s in range(SLOTS - 1, SLOTS + 2):
                step(Turn(R2, 0, s))

        def slot_live(s, late):
            return not isinstance(s.trip, int) or 0 <= s.off - late < SLOTS

        @block.sync
        def _(sp):
            def load_x(n):
                if n.has(R1):
                    sp.wait_ge(ln1_norm, (n - R1).count(LN1, LN1))
                sp.dma_start(xin[n.buf][:, :, :], x_v[bass.ds(n.number, 1), :, :, :].rearrange("b p i d -> (b p) i d")
                             if not isinstance(n.trip, int) else x_v[n.off]).then_inc(x_in[n.buf], 16)

            def load_res(n):
                if n.has(R1):
                    sp.wait_ge(resid_step, (n - R1).count(RES, RES))
                sp.dma_start(xres[n.buf][:, :, :], x_v[bass.ds(n.number, 1), :, :, :].rearrange("b p i d -> (b p) i d")
                             if not isinstance(n.trip, int) else x_v[n.off]).then_inc(res_in[n.buf], 16)

            load_x(Turn(R1, 0, 0))
            load_x(Turn(R1, 0, 1))
            load_res(Turn(R1, 0, 0))
            load_x(Turn(R1, 0, 2))
            for g in range(G):
                for v, src in enumerate((gate_d, up_d)):
                    sp.dma_start(wgu[:, g, v * EF:(v + 1) * EF].rearrange("p (e f) -> p e f", f=F),
                                 src[g * EPG:(g + 1) * EPG].rearrange("e p f -> p e f")).then_inc(e_in[g], 16)
                sp.dma_start(wd[:, g, :, :], down_d[g * EPG:(g + 1) * EPG].rearrange(
                    "e (c p) d -> p (e c) d", p=P)).then_inc(e_in[g], 16)
            sp.wait_ge(numbered, 1)
            for g in range(G - 1):
                sp.dma_start(scratch[G * REGION + g * P:G * REGION + (g + 1) * P, :], padrow[:, :]).then_inc(pad_out, 16)
            load_x(Turn(R1, 0, 3))
            load_res(Turn(R1, 0, 1))
            load_x(Turn(R1, 0, 4))
            load_res(Turn(R1, 0, 2))
            load_x(Turn(R1, 0, 5))
            with sp.Fori(1, 4) as trip:
                for r in range(R1):
                    load_res(Turn(R1, trip, r))
                    load_x(Turn(R1, trip, r + R1))
            for n in range(12, B):
                load_res(Turn(R1, 0, n))
                if n + R1 < B:
                    load_x(Turn(R1, 0, n + R1))

            def load_rows(s):
                if s.has(R2):
                    sp.wait_ge(out_sent[s.buf], (s - R2).round * 16 + 16)
                at = sp.value_load(slot_row[0:1, bass.ds(s.number, 1)], min_val=0, max_val=ROWS - P)
                sp.dma_start(rowin[s.buf][:, :], scratch[bass.ds(at, P), :]).then_inc(rows_in[s.buf], 16)

            sp.wait_ge(table, 1)
            for g in range(G):
                at = sp.value_load(padat[0:1, g:g + 1], min_val=g * REGION, max_val=g * REGION + T)
                sp.dma_start(scratch[bass.ds(at, P), :], padrow[:, :]).then_inc(padded, 16)

            sp.wait_ge(table, TABLE)
            sp.wait_ge(padded, 16 * G)
            sp.wait_ge(pad_out, 16 * (G - 1))
            for r in range(R1):
                sp.wait_ge(scattered[r], 16 * NT * ((B - 1 - r) // R1 + 1))
            for r in range(R2):
                load_rows(Turn(R2, 0, r))
            with sp.Fori(1, 8) as trip:
                for r in range(R2):
                    load_rows(Turn(R2, trip, r))
            for s in range(8 * R2, SLOTS):
                load_rows(Turn(R2, 0, s))

        @block.gpsimd
        def _(pool):
            for t in (ident, identb):
                nc.gpsimd.memset(t[:, :], 0.0).then_inc(consts, 1)
            pool.wait_ge(consts, 2)
            for t in (ident, identb):
                nc.gpsimd.affine_select(out=t[:, :], in_=t[:, :], compare_op=ALU.not_equal, fill=1.0, base=0,
                                        pattern=[[-1, P]], channel_multiplier=1).then_inc(consts, 1)
            nc.gpsimd.memset(trineg[:, :], 0.0).then_inc(consts, 1)
            nc.gpsimd.memset(before[:, :], 0.0).then_inc(consts, 1)
            pool.wait_ge(consts, 6)
            nc.gpsimd.affine_select(out=trineg[:, :], in_=trineg[:, :], compare_op=ALU.is_ge, fill=MASKED, base=0,
                                    pattern=[[1, P]], channel_multiplier=-1).then_inc(consts, 1)
            nc.gpsimd.affine_select(out=before[:, :], in_=before[:, :], compare_op=ALU.is_ge, fill=1.0, base=0,
                                    pattern=[[-1, P]], channel_multiplier=1).then_inc(consts, 1)
            nc.gpsimd.memset(ones[:, :], 1.0)
            nc.gpsimd.memset(halfneg[:, :], -0.5)
            for g in range(G):
                nc.gpsimd.memset(prefer[:, :, g], float(G - g))
                nc.gpsimd.memset(carry[0][:, g:g + 1], float(g * REGION // P))
            nc.gpsimd.memset(padrow[:, :], 0.0)
            for r in range(R1):
                last = nc.gpsimd.memset(row[r][:, :, RW - 4:RW], 0.0)
            last.then_inc(consts, 1)
            pool.wait_ge(consts, N_CONST)
            for r in range(R1):
                nc.gpsimd.iota(row[r][:, :, TOKEN].bitcast(I32), pattern=[[P, NT]], base=(r - R1) * S,
                               channel_multiplier=1)
            nc.gpsimd.iota(padrow[:, TOKEN:TOKEN + 1].bitcast(I32), pattern=[[0, 1]], base=T,
                           channel_multiplier=0).then_inc(numbered, 1)

            def deviations1(n):
                pool.wait_ge(ln1_stats, n.count(2 * NT, 2 * NT))
                if n.has(1):
                    pool.wait_ge(rstd1, n.count(RSTD1, 0))
                end_waits(pool)
                nc.gpsimd.tensor_scalar(vareps1[:, :], meanvar1[:, :, 1], LN_EPS, None, ALU.add).then_inc(rstd1, 1)
                nc.gpsimd.tensor_scalar(negmean1[:, :], meanvar1[:, :, 0], -1.0, None, ALU.mult).then_inc(rstd1, 1)
                pool.wait_ge(rstd1, n.count(RSTD1, 1))
                nc.gpsimd.tensor_tensor(norm1s[n.buf][:, :, 1], vareps1[:, :], halfneg[:, :], ALU.pow).then_inc(rstd1, 1)
                pool.wait_ge(rstd1, n.count(RSTD1, 3))
                nc.gpsimd.tensor_tensor(norm1s[n.buf][:, :, 0], negmean1[:, :], norm1s[n.buf][:, :, 1],
                                        ALU.mult).then_inc(rstd1, 1)

            def deviations2(n):
                pool.wait_ge(x1_step, n.count(X1, X1))
                if n.has(1):
                    pool.wait_ge(rstd2, n.count(RSTD2, 0))
                end_waits(pool)
                nc.gpsimd.tensor_scalar(vareps2[:, :], meanvar2[:, :, 1], LN_EPS, None, ALU.add).then_inc(rstd2, 1)
                nc.gpsimd.tensor_scalar(row[n.buf][:, :, NEGMEAN], meanvar2[:, :, 0], -1.0, None, ALU.mult).then_inc(rstd2, 1)
                pool.wait_ge(rstd2, n.count(RSTD2, 1))
                nc.gpsimd.tensor_tensor(row[n.buf][:, :, RSTD], vareps2[:, :], halfneg[:, :], ALU.pow).then_inc(rstd2, 1)

            def scatter(n):
                pool.wait_ge(place_step, n.count(2, 2))
                pool.wait_ge(route, n.count(ROUTE, ROUTE))
                pool.wait_ge(tokens_noted, n.count(1, 1))
                pool.wait_ge(rstd2, n.count(RSTD2, RSTD2))
                end_waits(pool)
                for i in range(NT):
                    nc.gpsimd.indirect_dma_start(
                        out=scratch, out_offset=bass.IndirectOffsetOnAxis(ap=place[n.buf][:, i:i + 1], axis=0),
                        in_=row[n.buf][:, i, :], in_offset=None).then_inc(scattered[n.buf], 16)

            def residual(n):
                pool.wait_ge(masked_found, n.count(1, 1))
                pool.wait_ge(vt_done, n.count(1, 1))
                if n.has(R1):
                    pool.wait_ge(x1_step, (n - R1).count(X1, X1))
                nc.gpsimd.tensor_tensor(resid[n.buf][:, :, :], vtot[n.buf][:, None, :].to_broadcast([P, NT, D]),
                                        u512[n.buf][:, :, None].to_broadcast([P, NT, D]), ALU.mult).then_inc(resid_step, 1)
                pool.wait_ge(res_in[n.buf], n.round * 16 + 16)
                pool.wait_ge(resid_step, n.count(RES, 1))
                nc.gpsimd.tensor_tensor(resid[n.buf][:, :, :], resid[n.buf][:, :, :], xres[n.buf][:, :, :],
                                        ALU.add).then_inc(resid_step, 1)

            def step(k):
                if live(k, 3):
                    deviations2(k - 3)
                if live(k, 2):
                    residual(k - 2)
                if live(k, -2):
                    deviations1(k + 2)
                if live(k, 4):
                    scatter(k - 4)
                if isinstance(k.trip, int) and k.off == 1:
                    nc.gpsimd.iota(tileat[:, :, :], pattern=[[REGION, G], [P, T // P]], base=0, channel_multiplier=0,
                                   allow_small_or_imprecise_dtypes=True)
                    nc.gpsimd.iota(slotno[:, :, :], pattern=[[0, G], [1, SLOTS]], base=0, channel_multiplier=0,
                                   allow_small_or_imprecise_dtypes=True).then_inc(slots_numbered, 1)

            attention_steps(pool, step)

            def normalise(s):
                pool.wait_ge(rows_in[s.buf], s.round * 16 + 16)
                if s.has(R2):
                    pool.wait_ge(yT_ready, (s - R2).count(1, 1))
                end_waits(pool)
                rt = rowin[s.buf]
                nc.gpsimd.tensor_scalar(yn[s.buf][:, :], rt[:, 0:D], rt[:, NEGMEAN:NEGMEAN + 1], rt[:, RSTD:RSTD + 1],
                                        ALU.add, ALU.mult).then_inc(yn_done, 1)

            def send(s):
                pool.wait_ge(out_done, s.count(1, 1))
                end_waits(pool)
                nc.gpsimd.indirect_dma_start(
                    out=out_d.rearrange("b s d -> (b s) d"),
                    out_offset=bass.IndirectOffsetOnAxis(ap=rowin[s.buf][:, TOKEN:TOKEN + 1].bitcast(I32), axis=0),
                    in_=outb[s.buf][:, :], in_offset=None, bounds_check=T - 1, oob_is_err=False
                ).then_inc(out_sent[s.buf], 16)

            AHEAD = 5
            for s in range(AHEAD):
                normalise(Turn(R2, 0, s))
            for s in range(R2 - AHEAD):
                normalise(Turn(R2, 0, s + AHEAD))
                send(Turn(R2, 0, s))
            with pool.Fori(0, 7) as trip:
                for r in range(R2):
                    normalise(Turn(R2, trip, R2 + r))
                    send(Turn(R2, trip, R2 - AHEAD + r))
            for s in range(8 * R2 - AHEAD, SLOTS):
                if s + AHEAD < SLOTS:
                    normalise(Turn(R2, 0, s + AHEAD))
                send(Turn(R2, 0, s))
            for r in range(R2):
                pool.wait_ge(out_sent[r], 16 * ((SLOTS - 1 - r) // R2 + 1))

        @block.scalar
        def _(act):
            act.dma_start(wqkv[:, :], w_d).then_inc(w_in, 16)
            act.dma_start(wrout[:, 0:G], macro_d).then_inc(r_in, 16)
            act.dma_start(wrout[:, G:NL].rearrange("p (g e) -> p g e", e=EPG),
                          micro_d.rearrange("g p e -> p g e")).then_inc(r_in, 16)
            for v, dst in enumerate((wqT, wkT)):
                act.wait_ge(wT_ready, 1)
                nc.scalar.activation(dst[:, :], ps_z[:, v * D:(v + 1) * D], ACT.Copy).then_inc(wT_done, 1)
            act.wait_ge(wqk_ready, 1)
            nc.scalar.activation(wqk[:, :], ps_s[0][:, 0:D], ACT.Copy).then_inc(wqk_done, 1)

            def softmax_exp(n, i):
                act.wait_ge(s_masked, n.count(NT, i + 1))
                nc.scalar.activation(probs[n.buf][:, OFF[i]:OFF[i] + WIDTH[i]], negs[i % 2][:, 0:WIDTH[i]], ACT.Exp,
                                     bias=negmax[n.buf][:, i:i + 1], scale=-1.0,
                                     accum_out=psums[n.buf][:, i:i + 1]).then_inc(p_done, 1)

            def copy_probsT(n, m):
                act.wait_ge(pT_ready, n.count(NT, m + 1))
                w = S - m * P
                nc.scalar.activation(probsT[m][:, 0:w], ps_pt[m % 2][:, 0:w], ACT.Copy).then_inc(pT_done, 1)

            def copy_x2T(n):
                act.wait_ge(x2T_ready, n.count(1, 1))
                nc.scalar.activation(x2T[:, :], ps_tr[:, :], ACT.Copy).then_inc(x2T_done, 1)

            def exp_logits(n):
                act.wait_ge(log_ready, n.count(1, 1))
                if n.has(1):
                    act.wait_ge(route, (n - 1).count(ROUTE, 1))
                nc.scalar.activation(elog[:, :, :], ps_log, ACT.Exp, scale=-1.0).then_inc(exp_done, 1)

            def copy_zT(n):
                act.wait_ge(z_ready, n.count(1, 1))
                nc.scalar.activation(zT[:, :], ps_z[:, :], ACT.Copy).then_inc(z_done, 1)

            def copy_xT(n):
                act.wait_ge(xT_ready, n.count(1, 1))
                nc.scalar.activation(xnT[n.buf][:, :], ps_tr[:, :], ACT.Copy,
                                     accum_out=xsum[n.buf][:, :]).then_inc(xT_done, 1)

            def copy_vtot(n):
                act.wait_ge(vt_ready, n.count(1, 1))
                if n.has(R1):
                    act.wait_ge(resid_step, (n - R1).count(RES, RES))
                nc.scalar.activation(vtot[n.buf][:, :], ps_vtot, ACT.Copy).then_inc(vt_done, 1)

            def upper_weights(g):
                act.wait_ge(e_in[g], 16 * 3)
                nc.scalar.activation(wguh[:, g, :], wgu[:, g, :], ACT.Copy).then_inc(wh_done, 1)
                nc.scalar.activation(wds[:, g, :, 0, :], wd[:, g, :, :], ACT.Copy).then_inc(wh_done, 1)

            def norm1(n, tiles):
                act.wait_ge(rstd1, n.count(RSTD1, RSTD1))
                if n.has(R1):
                    act.wait_ge(z_ready, (n - R1).count(1, 1))
                for i in tiles:
                    nc.scalar.activation(xn[n.buf][:, i, :], xin[n.buf][:, i, :], ACT.Identity,
                                         bias=norm1s[n.buf][:, i, 0:1], scale=norm1s[n.buf][:, i, 1:2]).then_inc(ln1_norm, 1)

            def copy_q(n):
                act.wait_ge(q_ready, n.count(1, 1))
                nc.scalar.activation(qT[n.buf][:, :], ps_o[:, :], ACT.Copy).then_inc(q_done, 1)

            def step(k):
                if isinstance(k.trip, int) and k.off == B + 2:
                    upper_weights(2)
                    upper_weights(3)
                if live(k, 2):
                    copy_probsT(k - 2, 0)
                    copy_probsT(k - 2, 1)
                if live(k, 0):
                    copy_xT(k)
                if live(k, 1):
                    copy_vtot(k - 1)
                    softmax_exp(k - 1, 0)
                if live(k, 2):
                    copy_probsT(k - 2, 2)
                    copy_probsT(k - 2, 3)
                if live(k, 0):
                    copy_q(k)
                if live(k, 2):
                    copy_zT(k - 2)
                if live(k, 3):
                    copy_x2T(k - 3)
                if live(k, 1):
                    softmax_exp(k - 1, 1)
                    softmax_exp(k - 1, 2)
                if live(k, -1):
                    norm1(k + 1, (0, 1))
                if live(k, 3):
                    exp_logits(k - 3)
                if live(k, 1):
                    softmax_exp(k - 1, 3)
                if live(k, -1):
                    norm1(k + 1, (2, 3))
                if isinstance(k.trip, int) and k.off in (0, 1):
                    upper_weights(k.off)

            attention_steps(act, step)

            act.wait_ge(consts, N_CONST)
            nc.scalar.activation(silu_first[:, :], ones[:, 0:1], ACT.Silu)

            def step2(s):
                if slot_live(s, -1):
                    n = s + 1
                    act.wait_ge(yT_ready, n.count(1, 1))
                    if n.has(2):
                        act.wait_ge(u_ready, (n - 2).count(1, 1))
                    nc.scalar.activation(yh[n.buf % 2][:, :], ps_y[:, 0:P], ACT.Copy).then_inc(yh_done, 1)
                if slot_live(s, 0):
                    act.wait_ge(g_ready, s.count(1, 1))
                    if s.has(2):
                        act.wait_ge(h_done, (s - 2).count(EPG, EPG))
                    nc.scalar.activation(act_g[s.buf % 2][:, :], ps_g[s.buf % 2][:, :], ACT.Silu).then_inc(silu_done, 1)
                if slot_live(s, 1):
                    n = s - 1
                    act.wait_ge(hT_ready, n.count(1, 1))
                    if n.has(2):
                        act.wait_ge(y_ready, (n - 2).count(1, 1))
                    nc.scalar.activation(hh[n.buf % 2][:, :], ps_ht[:, :], ACT.Copy).then_inc(hh_done, 1)

            expert_steps(act, step2)

        @block.vector
        def _(dve):
            def place_rows(n):
                dve.wait_ge(pos_ready, n.count(1, 1))
                nc.vector.tensor_tensor(posm[:, :, :], ps_pos, pick[n.buf][:, :, :], ALU.mult).then_inc(place_step, 1)
                yield
                dve.wait_ge(place_step, n.count(2, 1))
                with nc.allow_low_precision(reason="whole numbers below 2**24, summed in float32"):
                    nc.vector.tensor_reduce(out=place[n.buf][:, :], in_=posm[:, :, :], op=ALU.add,
                                            axis=AX.X).then_inc(place_step, 1)
                yield

            def mask_scores(n, i):
                dve.wait_ge(s_ready, n.count(NT, i + 1))
                w = WIDTH[i]
                nc.vector.tensor_scalar(zmask[i % 2][:, 0:w], ps_s[i % 2][:, 0:w], 0.0, MASKED, ALU.is_equal,
                                        ALU.mult).then_inc(zero_found, 1)
                yield
                dve.wait_ge(zero_found, n.count(NT, i + 1))
                if n.has(1) or i >= 2:
                    dve.wait_ge(p_done, n.count(NT, i - 1))
                end_waits(dve)
                nc.vector.tensor_tensor_reduce(out=negs[i % 2][:, 0:w], in0=ps_s[i % 2][:, 0:w],
                                               in1=zmask[i % 2][:, 0:w], scale=-SCALE, scalar=3.0e38,
                                               op0=ALU.add, op1=ALU.min,
                                               accum_out=negmax[n.buf][:, i:i + 1]).then_inc(s_masked, 1)
                yield

            def find_masked(n):
                dve.wait_ge(s_masked, n.count(NT, NT))
                if n.has(R1):
                    dve.wait_ge(resid_step, (n - R1).count(RES, 1))
                nc.vector.tensor_scalar(u512[n.buf][:, :], negmax[n.buf][:, :], ALL_MASKED, 1.0 / S, ALU.is_gt,
                                        ALU.mult).then_inc(masked_found, 1)
                yield

            def count(n):
                dve.wait_ge(route, n.count(ROUTE, 7))
                with nc.allow_low_precision(reason="whole numbers below 2048"):
                    nc.vector.tensor_reduce(out=four[:, :], in_=pick[n.buf][:, :, :].rearrange("p i g -> p g i"),
                                            op=ALU.add, axis=AX.X).then_inc(counted, 1)
                yield
                dve.wait_ge(counted, n.count(COUNT, 1))
                nc.vector.tensor_tensor(carry[(n + 1).buf][:, :], carry[n.buf][:, :], four[:, :], ALU.add).then_inc(counted, 1)
                yield

            def stats1(n):
                dve.wait_ge(x_in[n.buf], n.round * 16 + 16)
                if n.has(1):
                    dve.wait_ge(ln1_stats, n.count(2 * NT, 0))
                for i in range(NT):
                    nc.vector.bn_stats(st1[:, i, :], xin[n.buf][:, i, :]).then_inc(ln1_stats, 1)
                    yield
                dve.wait_ge(ln1_stats, n.count(2 * NT, NT))
                if n.has(1):
                    dve.wait_ge(rstd1, (n - 1).count(RSTD1, 2))
                end_waits(dve)
                for i in range(NT):
                    nc.vector.bn_aggr(meanvar1[:, i, :], st1[:, i, :]).then_inc(ln1_stats, 1)
                    yield

            def norm2(n):
                dve.wait_ge(rstd2, n.count(RSTD2, RSTD2))
                if n.has(R1):
                    dve.wait_ge(x2T_ready, (n - R1).count(1, 1))
                for i in range(NT):
                    nc.vector.tensor_scalar(xn2[n.buf][:, i, :], row[n.buf][:, i, 0:D], row[n.buf][:, i, NEGMEAN:NEGMEAN + 1],
                                            row[n.buf][:, i, RSTD:RSTD + 1], ALU.add, ALU.mult).then_inc(ln2_norm, 1)
                    yield

            def new_x(n):
                dve.wait_ge(p_done, n.count(NT, NT))
                nc.vector.reciprocal(rsum[:, :], psums[n.buf][:, :]).then_inc(x1_step, 1)
                yield
                dve.wait_ge(x1_step, n.count(X1, 1))
                nc.vector.scalar_tensor_tensor(out=rlive[:, :], in0=negmax[n.buf][:, :], scalar=ALL_MASKED,
                                               in1=rsum[:, :], op0=ALU.is_le, op1=ALU.mult).then_inc(x1_step, 1)
                yield
                if n.has(R1):
                    dve.wait_ge(scattered[n.buf], (n - R1).round * 16 * NT + 16 * NT)
                end_waits(dve)
                ids = row[n.buf][:, :, TOKEN].bitcast(I32)
                nc.vector.tensor_scalar(ids, ids, float(R1 * S), None, ALU.add).then_inc(tokens_noted, 1)
                yield
                dve.wait_ge(x1_step, n.count(X1, 2))
                dve.wait_ge(resid_step, n.count(RES, RES))
                dve.wait_ge(o_ready, n.count(1, 1))
                for i in range(NT):
                    nc.vector.scalar_tensor_tensor(out=row[n.buf][:, i, 0:D], in0=ps_o[:, i * D:(i + 1) * D],
                                                   scalar=rlive[:, i:i + 1], in1=resid[n.buf][:, i, :],
                                                   op0=ALU.mult, op1=ALU.add).then_inc(x1_step, 1)
                    yield
                dve.wait_ge(x1_step, n.count(X1, 2 + NT))
                for i in range(NT):
                    nc.vector.bn_stats(st2[:, i, :], row[n.buf][:, i, 0:D]).then_inc(x1_step, 1)
                    yield
                dve.wait_ge(x1_step, n.count(X1, 2 + 2 * NT))
                if n.has(1):
                    dve.wait_ge(rstd2, (n - 1).count(RSTD2, 2))
                end_waits(dve)
                for i in range(NT):
                    nc.vector.bn_aggr(meanvar2[:, i, :], st2[:, i, :]).then_inc(x1_step, 1)
                    yield

            def routed(n, done):
                dve.wait_ge(route, n.count(ROUTE, done))

            def pick_group(n):
                def after(done):
                    routed(n, done)

                dve.wait_ge(exp_done, n.count(1, 1))
                nc.vector.tensor_scalar(elog1[:, :, :], elog[:, :, :], 1.0, None, ALU.add).then_inc(route, 1)
                yield
                after(1)
                nc.vector.reciprocal(sig[:, :, :], elog1[:, :, :]).then_inc(route, 1)
                yield
                after(2)
                nc.vector.tensor_reduce(out=top[:, :], in_=sig[:, :, 0:G], op=ALU.max, axis=AX.X).then_inc(route, 1)
                yield
                after(3)
                nc.vector.tensor_tensor(istop[:, :, :], sig[:, :, 0:G], top[:, :, None].to_broadcast([P, NT, G]),
                                        ALU.is_equal).then_inc(route, 1)
                yield
                after(4)
                nc.vector.tensor_tensor(rank[:, :, :], istop[:, :, :], prefer[:, :, :], ALU.mult).then_inc(route, 1)
                yield
                after(5)
                nc.vector.tensor_reduce(out=toprank[:, :], in_=rank[:, :, :], op=ALU.max, axis=AX.X).then_inc(route, 1)
                yield
                after(6)
                nc.vector.tensor_tensor(pick[n.buf][:, :, :], rank[:, :, :],
                                        toprank[:, :, None].to_broadcast([P, NT, G]), ALU.is_equal).then_inc(route, 1)
                yield

            def pick_experts(n):
                def after(done):
                    routed(n, done)

                after(7)
                nc.vector.tensor_tensor(micro[:, :, :, :], sig[:, :, G:NL].rearrange("p i (g e) -> p i g e", e=EPG),
                                        pick[n.buf][:, :, :, None].to_broadcast([P, NT, G, EPG]),
                                        ALU.mult).then_inc(route, 1)
                nc.vector.tensor_scalar(tope[:, :], top[:, :], TOP_EPS, None, ALU.add).then_inc(route, 1)
                yield
                after(9)
                nc.vector.tensor_reduce(out=msel[:, :, :], in_=micro[:, :, :, :].rearrange("p i g e -> p i e g"),
                                        op=ALU.add, axis=AX.X).then_inc(route, 1)
                yield
                after(10)
                nc.vector.tensor_tensor(msum[:, :], msel[:, :, 0], msel[:, :, 1], ALU.add).then_inc(route, 1)
                yield
                after(11)
                nc.vector.scalar_tensor_tensor(out=wden[:, :], in0=msum[:, :], scalar=TOP_EPS, in1=tope[:, :],
                                               op0=ALU.add, op1=ALU.mult).then_inc(route, 1)
                yield
                after(12)
                nc.vector.reciprocal(wrec[:, :], wden[:, :]).then_inc(route, 1)
                yield
                after(13)
                nc.vector.tensor_tensor(wtop[:, :], wrec[:, :], top[:, :], ALU.mult).then_inc(route, 1)
                yield
                after(14)
                nc.vector.tensor_tensor(row[n.buf][:, :, WGT:WGT + EPG], msel[:, :, :],
                                        wtop[:, :, None].to_broadcast([P, NT, EPG]), ALU.mult).then_inc(route, 1)
                yield

            def lower_weights(g):
                dve.wait_ge(wh_done, 2 * g + 1)
                nc.vector.tensor_tensor(wgul[:, g, :], wgu[:, g, :], wguh[:, g, :].bitcast(F32),
                                        ALU.subtract).then_inc(wl_done, 1)
                dve.wait_ge(wh_done, 2 * g + 2)
                nc.vector.tensor_tensor(wds[:, g, :, 1, :], wd[:, g, :, :], wds[:, g, :, 0, :].bitcast(F32),
                                        ALU.subtract).then_inc(wl_done, 1)

            ORDER = "r s r s r s r s r 0 r s s 0 r s s c m w m w m c w m w 1 w p 1 w p 2 w x x 2 x x x x x 3 x x 3 x x u x x x x"

            def step(k):
                if isinstance(k.trip, int) and k.off == 0:
                    dve.wait_ge(consts, N_CONST)
                    dve.wait_ge(numbered, 1)
                kinds = {"p": (4, lambda: place_rows(k - 4)), "m": (3, lambda: norm2(k - 3)),
                         "u": (1, lambda: find_masked(k - 1)), "s": (-2, lambda: stats1(k + 2)), "r": (4, lambda: pick_group(k - 4)), "c": (4, lambda: count(k - 4)), "w": (4, lambda: pick_experts(k - 4)), "x": (2, lambda: new_x(k - 2))}
                for i in range(NT):
                    kinds[str(i)] = (1, lambda i=i: mask_scores(k - 1, i))
                going = {c: make() for c, (late, make) in kinds.items() if live(k, late)}
                for c in ORDER.split():
                    if c in going:
                        next(going[c], None)
                if isinstance(k.trip, int) and k.off in (0, 1):
                    lower_weights(k.off)

            attention_steps(dve, step)

            def after(done):
                dve.wait_ge(table, done)

            dve.wait_ge(end_ready, 1)
            dve.wait_ge(slots_numbered, 1)
            nc.vector.tensor_copy(padat[:, :], ps_end[0:1, :]).then_inc(table, 1)
            nc.vector.tensor_copy(ends[:, :], ps_end[0:1, :]).then_inc(table, 1)
            after(2)
            nc.vector.tensor_tensor(tilehit[:, :, :], tileat[:, :, :], ends[:, :, None].to_broadcast([1, G, T // P]),
                                    ALU.is_lt).then_inc(table, 1)
            after(3)
            nc.vector.tensor_reduce(out=tiles[:, :], in_=tilehit[:, :, :], op=ALU.add, axis=AX.X).then_inc(table, 1)
            after(4)
            nc.vector.tensor_scalar(skip[:, :], tiles[:, :], -float(P), float(REGION), ALU.mult, ALU.add).then_inc(table, 1)
            nc.vector.tensor_tensor_scan(out=tcum[:, :], data0=ones[0:1, 0:G], data1=tiles[:, :], initial=0.0,
                                         op0=ALU.mult, op1=ALU.add).then_inc(table, 1)
            after(6)
            nc.vector.tensor_tensor(past[:, :, :], slotno[:, :, :], tcum[:, :, None].to_broadcast([1, G, SLOTS]),
                                    ALU.is_ge).then_inc(table, 1)
            after(7)
            nc.vector.tensor_tensor(pastskip[:, :, :], past[:, :, :], skip[:, :, None].to_broadcast([1, G, SLOTS]),
                                    ALU.mult).then_inc(table, 1)
            nc.vector.tensor_reduce(out=grp_f[:, :], in_=past[:, :, :].rearrange("p g s -> p s g"), op=ALU.add,
                                    axis=AX.X).then_inc(table, 1)
            after(9)
            nc.vector.tensor_scalar(slot_group[:, :], grp_f[:, :], float(G - 1), None, ALU.min).then_inc(table, 1)
            nc.vector.tensor_reduce(out=rowsum[:, :], in_=pastskip[:, :, :].rearrange("p g s -> p s g"), op=ALU.add,
                                    axis=AX.X).then_inc(table, 1)
            after(11)
            nc.vector.scalar_tensor_tensor(out=slot_row[:, :], in0=slotno[:, 0, :], scalar=float(P), in1=rowsum[:, :],
                                           op0=ALU.mult, op1=ALU.add).then_inc(table, 1)
            lower_weights(2)
            lower_weights(3)

            def step2(s):
                if slot_live(s, -1):
                    n = s + 1
                    dve.wait_ge(yh_done, n.count(1, 1))
                    nc.vector.tensor_tensor(yl[n.buf % 2][:, :], ps_y[:, 0:P], yh[n.buf % 2][:, :].bitcast(F32),
                                            ALU.subtract).then_inc(yl_done, 1)
                if slot_live(s, 1):
                    n = s - 1
                    dve.wait_ge(hh_done, n.count(1, 1))
                    nc.vector.tensor_tensor(hl[n.buf % 2][:, :], ps_ht[:, :], hh[n.buf % 2][:, :].bitcast(F32),
                                            ALU.subtract).then_inc(hl_done, 1)
                if slot_live(s, 0):
                    dve.wait_ge(silu_done, s.count(1, 1))
                    dve.wait_ge(u_ready, s.count(1, 1))
                    if s.has(2):
                        dve.wait_ge(hT_ready, (s - 2).count(1, 1))
                    for e in range(EPG):
                        nc.vector.scalar_tensor_tensor(
                            out=hid[s.buf % 2][:, e * F:(e + 1) * F], in0=act_g[s.buf % 2][:, e * F:(e + 1) * F],
                            scalar=rowin[s.buf][:, WGT + e:WGT + e + 1], in1=ps_u[s.buf % 2][:, e * F:(e + 1) * F],
                            op0=ALU.mult, op1=ALU.mult).then_inc(h_done, 1)
                if slot_live(s, 2):
                    n = s - 2
                    dve.wait_ge(y_ready, n.count(1, 1))
                    if n.has(R2):
                        dve.wait_ge(out_sent[n.buf], (n - R2).round * 16 + 16)
                    nc.vector.tensor_tensor(outx[:, :], ps_out[:, D:2 * D], rowin[n.buf][:, 0:D], ALU.add).then_inc(out_part, 1)
                    dve.wait_ge(out_part, n.count(1, 1))
                    nc.vector.tensor_tensor(outb[n.buf][:, :], ps_out[:, 0:D], outx[:, :], ALU.add).then_inc(out_done, 1)

            expert_steps(dve, step2)

        @block.tensor
        def _(pe):
            pe.wait_ge(w_in, 16)
            pe.wait_ge(consts, N_CONST)
            nc.tensor.transpose(ps_z[:, 0:D], wqkv[:, 0:D], ident[:, :])
            nc.tensor.transpose(ps_z[:, D:2 * D], wqkv[:, D:2 * D], ident[:, :]).then_inc(wT_ready, 1)
            pe.wait_ge(wT_done, 2)
            nc.tensor.matmul(ps_s[0][:, 0:D], wqT[:, :], wkT[:, :], start=True, stop=True).then_inc(wqk_ready, 1)
            pe.wait_ge(wqk_done, 1)
            pe.wait_ge(r_in, 32)

            def positions(n):
                pe.wait_ge(route, n.count(ROUTE, 7))
                if n.has(1):
                    pe.wait_ge(counted, (n - 1).count(COUNT, COUNT))
                if live(n, -3):
                    pe.wait_ge(vt_done, (n + 3).count(1, 1))
                pk = pick[n.buf]
                nc.tensor.matmul(ps_pos, before[:, :], pk[:, :, :], start=True, stop=False)
                nc.tensor.matmul(ps_pos, ones[:, :], carry[n.buf][:, None, :].to_broadcast([P, NT, G]),
                                 start=False, stop=False)
                for i in range(NT - 1):
                    last = nc.tensor.matmul(ps_pos[:, i + 1:NT, :], ones[:, :],
                                            pk[:, i:i + 1, :].to_broadcast([P, NT - 1 - i, G]),
                                            start=False, stop=i == NT - 2)
                last.then_inc(pos_ready, 1)

            def scores(n, i):
                pe.wait_ge(q_done, n.count(1, 1))
                if n.has(1) or i >= 2:
                    pe.wait_ge(s_masked, n.count(NT, i - 1))
                nc.tensor.matmul(ps_s[i % 2][:, 0:WIDTH[i]], qT[n.buf][:, i * P:(i + 1) * P],
                                 xnT[n.buf][:, i * P:S], start=True, stop=False)
                nc.tensor.matmul(ps_s[i % 2][:, 0:P], identb[:, :], trineg[:, :],
                                 start=False, stop=True).then_inc(s_ready, 1)

            def transpose_probs(n, m):
                pe.wait_ge(p_done, n.count(NT, NT))
                if n.has(1) or m >= 2:
                    pe.wait_ge(pT_done, n.count(NT, m - 1))
                j = NT - 1 - m
                for i in range(j + 1):
                    at = OFF[i] + (j - i) * P
                    last = nc.tensor.transpose(ps_pt[m % 2][:, i * P:(i + 1) * P], probs[n.buf][:, at:at + P], ident[:, :])
                last.then_inc(pT_ready, 1)

            def weigh(n, m):
                pe.wait_ge(pT_done, n.count(NT, m + 1))
                if m == 0 and n.has(1):
                    pe.wait_ge(z_done, n.count(1, 0))
                j = NT - 1 - m
                mm = nc.tensor.matmul(ps_z[:, 0:(j + 1) * P], xn[n.buf][:, j, :], probsT[m][:, 0:(j + 1) * P],
                                      start=m == 0, stop=m == NT - 1)
                if m == NT - 1:
                    mm.then_inc(z_ready, 1)

            def transpose_x2(n):
                pe.wait_ge(ln2_norm, n.count(LN2, LN2))
                if live(n, -3):
                    pe.wait_ge(xT_done, (n + 3).count(1, 1))
                elif n.has(1):
                    pe.wait_ge(x2T_done, n.count(1, 0))
                for i in range(NT):
                    last = nc.tensor.transpose(ps_tr[:, i * P:(i + 1) * P], xn2[n.buf][:, i, :], ident[:, :])
                last.then_inc(x2T_ready, 1)

            def logits(n):
                pe.wait_ge(x2T_done, n.count(1, 1))
                if n.has(1):
                    pe.wait_ge(place_step, (n - 1).count(2, 1))
                else:
                    pe.wait_ge(vt_done, (n + 2).count(1, 1))
                for i in range(NT):
                    last = nc.tensor.matmul(ps_log[:, i, :], x2T[:, i * P:(i + 1) * P], wrout[:, :],
                                            start=True, stop=True)
                last.then_inc(log_ready, 1)

            def transpose_x(n):
                pe.wait_ge(ln1_norm, n.count(LN1, LN1))
                if n.has(4):
                    pe.wait_ge(x2T_done, (n - 4).count(1, 1))
                elif n.has(1):
                    pe.wait_ge(xT_done, n.count(1, 0))
                for i in range(NT):
                    last = nc.tensor.transpose(ps_tr[:, i * P:(i + 1) * P], xn[n.buf][:, i, :], ident[:, :])
                last.then_inc(xT_ready, 1)

            def queries(n):
                pe.wait_ge(xT_done, n.count(1, 1))
                if n.has(3):
                    pe.wait_ge(x1_step, (n - 3).count(X1, 2 + NT))
                elif n.has(1):
                    pe.wait_ge(q_done, n.count(1, 0))
                nc.tensor.matmul(ps_o[:, :], wqk[:, :], xnT[n.buf][:, :], start=True, stop=True).then_inc(q_ready, 1)

            def value_total(n):
                if n.has(3):
                    pe.wait_ge(exp_done, (n - 3).count(1, 1))
                nc.tensor.matmul(ps_vtot, xsum[n.buf][:, 0:1].to_broadcast([P, P]), wqkv[:, 2 * D:3 * D],
                                 start=True, stop=True).then_inc(vt_ready, 1)

            def attend(n):
                pe.wait_ge(z_done, n.count(1, 1))
                if live(n, -2):
                    pe.wait_ge(q_done, (n + 2).count(1, 1))
                else:
                    pe.wait_ge(x1_step, (n - 1).count(X1, 2 + NT))
                for i in range(NT):
                    last = nc.tensor.matmul(ps_o[:, i * D:(i + 1) * D], zT[:, i * P:(i + 1) * P],
                                            wqkv[:, 2 * D:3 * D], start=True, stop=True)
                last.then_inc(o_ready, 1)

            def step(k):
                if live(k, 1):
                    scores(k - 1, 0)
                if live(k, 2):
                    transpose_probs(k - 2, 0)
                    transpose_probs(k - 2, 1)
                if live(k, 0):
                    transpose_x(k)
                if live(k, 1):
                    value_total(k - 1)
                if live(k, 2):
                    weigh(k - 2, 0)
                if live(k, 1):
                    scores(k - 1, 1)
                if live(k, 2):
                    transpose_probs(k - 2, 2)
                    transpose_probs(k - 2, 3)
                    weigh(k - 2, 1)
                if live(k, 0):
                    queries(k)
                if live(k, 2):
                    weigh(k - 2, 2)
                    weigh(k - 2, 3)
                if live(k, 4):
                    positions(k - 4)
                if live(k, 3):
                    transpose_x2(k - 3)
                if live(k, 1):
                    scores(k - 1, 2)
                if live(k, 2):
                    attend(k - 2)
                if live(k, 1):
                    scores(k - 1, 3)
                if live(k, 3):
                    logits(k - 3)

            attention_steps(pe, step)

            pe.wait_ge(counted, B * COUNT)
            pe.wait_ge(place_step, 2 * B)
            nc.tensor.matmul(ps_end, ones[:, :], carry[B % R1][:, :], start=True, stop=True).then_inc(end_ready, 1)

            pe.wait_ge(wl_done, 2 * G)
            pe.wait_ge(table, TABLE)

            def group_of(s):
                return pe.value_load(slot_group[0:1, bass.ds(s.number, 1)], min_val=0, max_val=G - 1)

            def split_matmul(out, hi, lo, whi, wlo, start, stop):
                nc.tensor.matmul(out, hi, whi, start=start, stop=False)
                nc.tensor.matmul(out, hi, wlo, start=False, stop=False)
                return nc.tensor.matmul(out, lo, whi, start=False, stop=stop)

            loaded = {}

            def step2(s):
                if slot_live(s, 0):
                    pe.wait_ge(yl_done, s.count(1, 1))
                    g = loaded[isinstance(s.trip, int), s.off] = group_of(s)
                if slot_live(s, -1):
                    n = s + 1
                    pe.wait_ge(yn_done, n.count(1, 1))
                    nc.tensor.transpose(ps_y[:, 0:P], yn[n.buf][:, :], ident[:, :]).then_inc(yT_ready, 1)
                if slot_live(s, 0):
                    b = s.buf % 2
                    split_matmul(ps_g[b][:, :], yh[b][:, :], yl[b][:, :],
                                 wguh[:, bass.ds(g, 1), 0:EF].rearrange("p g f -> p (g f)"),
                                 wgul[:, bass.ds(g, 1), 0:EF].rearrange("p g f -> p (g f)"),
                                 True, True).then_inc(g_ready, 1)
                if slot_live(s, 2):
                    here = isinstance(s.trip, int), s.off - 2
                    gd = loaded[here] if here in loaded else group_of(s - 2)
                if slot_live(s, 2):
                    pe.wait_ge(hl_done, (s - 2).count(1, 1))
                if slot_live(s, 1):
                    n = s - 1
                    pe.wait_ge(h_done, n.count(EPG, EPG))
                    for c in range(NC):
                        last = nc.tensor.transpose(ps_ht[:, c * P:(c + 1) * P], hid[n.buf % 2][:, c * P:(c + 1) * P],
                                                   ident[:, :])
                    last.then_inc(hT_ready, 1)
                if slot_live(s, 0):
                    split_matmul(ps_u[b][:, :], yh[b][:, :], yl[b][:, :],
                                 wguh[:, bass.ds(g, 1), EF:2 * EF].rearrange("p g f -> p (g f)"),
                                 wgul[:, bass.ds(g, 1), EF:2 * EF].rearrange("p g f -> p (g f)"),
                                 True, True).then_inc(u_ready, 1)
                if slot_live(s, 2):
                    n = s - 2
                    if n.has(1):
                        pe.wait_ge(out_done, n.count(1, 0))
                    for c in range(NC):
                        up = hh[n.buf % 2][:, c * P:(c + 1) * P], hl[n.buf % 2][:, c * P:(c + 1) * P]
                        wdc = wds[:, bass.ds(gd, 1), c, :, :].rearrange("p g v d -> p (g v) d")
                        if c == NC - 1:
                            nc.tensor.matmul(ps_out[:, 0:D], up[1], wdc[:, 0, :], start=False, stop=False)
                        last = nc.tensor.matmul(ps_out[:, 0:2 * D], up[0], wdc, start=c == 0, stop=c == NC - 1)
                        if c < NC - 1:
                            nc.tensor.matmul(ps_out[:, 0:D], up[1], wdc[:, 0, :], start=False, stop=False)
                    last.then_inc(y_ready, 1)

            expert_steps(pe, step2)


_INS = ['L0_attn_x', 'L0_attn_W', 'L0_ffn_macro_w', 'L0_ffn_micro_w', 'L0_ffn_gate_w', 'L0_ffn_up_w', 'L0_ffn_down_w']
_OUTS = [((16, 512, 128), 'float32')]


def kernel(**inputs):
    import numpy as _np
    import concourse.bacc as _bacc
    from concourse import mybir as _mybir
    from concourse.bass_utils import run_bass_kernel_spmd as _run

    nc = _bacc.Bacc("TRN2", target_bir_lowering=False, num_devices=1)
    arrays, args = {}, []
    for name in _INS:
        a = _np.ascontiguousarray(inputs[name])
        arrays[f"in_{name}_dram"] = a
        args.append(nc.dram_tensor(f"in_{name}_dram", a.shape, _mybir.dt.from_np(a.dtype), kind="ExternalInput").ap())
    for i, (shape, dtype) in enumerate(_OUTS):
        dt = _mybir.dt.from_np(_np.dtype(dtype))
        args.append(nc.dram_tensor(f"out_{i}_dram", shape, dt, kind="ExternalOutput").ap())
    preln_attention_moe_kernel(nc, *args)
    r = _run(nc, [arrays], core_ids=[0])
    got = tuple(r.results[0][f"out_{i}_dram"] for i in range(len(_OUTS)))
    return got[0]
```

```python
import concourse.bass as bass
from concourse import mybir
from contextlib import ExitStack

F32 = mybir.dt.float32
F32R = mybir.dt.float32r
BF16 = mybir.dt.bfloat16
F16 = mybir.dt.float16
I32 = mybir.dt.int32
ALU = mybir.AluOpType
ACT = mybir.ActivationFunctionType
AX = mybir.AxisListType

P = 128


class Turn:

    def __init__(self, ring, trip, off):
        self.ring, self.trip, self.off = ring, trip, off
        self.buf = off % ring
        self.number = off if isinstance(trip, int) else ring * trip + off
        self.round = off // ring if isinstance(trip, int) else trip + off // ring

    def __add__(self, d):
        return Turn(self.ring, self.trip, self.off + d)

    def __sub__(self, d):
        return self + -d

    def has(self, earlier):
        return not isinstance(self.trip, int) or self.off >= earlier

    def count(self, per, more):
        return self.number * per + more


def preln_attention_moe_kernel(nc, x_d, w_d, macro_d, micro_d, gate_d, up_d, down_d, out_d):
    B, S, D = x_d.shape
    NT = S // P
    T = B * S
    G, _, EPG = micro_d.shape
    F = gate_d.shape[2]
    EF = EPG * F
    NC = EF // P
    NL = G + G * EPG
    SCALE = 1.0 / float(D) ** 0.5
    MASKED = -2.0 ** 53
    ALL_MASKED = 1e14
    LN_EPS, TOP_EPS = 1e-5, 1e-9
    WIDTH = [S - P * i for i in range(NT)]
    OFF = [sum(WIDTH[:i]) for i in range(NT)]
    SW = sum(WIDTH)
    NEGMEAN, RSTD, WGT, TOKEN, RW = D, D + 1, D + 2, D + 4, D + 8
    REGION = T + P
    SLOTS = T // P + G - 1
    ROWS = G * REGION + (G - 1) * P
    R1 = 3
    R2 = 8
    STEPS = [list(range(-2, 6)), (2, 4), list(range(12, 20))]
    assert B == 16 and NT == 4 and R1 * 5 + 1 == B and SLOTS == 67

    scratch = nc.dram_tensor("sorted_rows", [ROWS, RW], F32).ap()

    ctx = ExitStack()
    with ctx:
        def sb(name, shape, dt=F32):
            return ctx.enter_context(nc.sbuf_tensor(name, shape, dt))

        def sem(name):
            return ctx.enter_context(nc.semaphore(name))

        ident = sb("ident", [P, P])
        identb = sb("identb", [P, P], BF16)
        trineg = sb("trineg", [P, P], BF16)
        before = sb("before", [P, P], F16)
        ones = sb("ones", [P, P], F16)
        halfneg = sb("halfneg", [P, NT])
        prefer = sb("prefer", [P, NT, G])
        padrow = sb("padrow", [P, RW])
        wqkv = sb("wqkv", [P, 3 * D])
        wqT = sb("wqT", [P, D])
        wkT = sb("wkT", [P, D])
        wqk = sb("wqk", [P, D])
        wrout = sb("wrout", [P, NL])
        wgu = sb("wgu", [P, G, 2 * EF])
        wguh = sb("wguh", [P, G, 2 * EF], F32R)
        wgul = sb("wgul", [P, G, 2 * EF], F32R)
        wd = sb("wd", [P, G, NC, D])
        wds = sb("wds", [P, G, NC, 2, D], F32R)
        xin = [sb(f"xin{r}", [P, NT, D]) for r in range(R1)]
        xres = [sb(f"xres{r}", [P, NT, D]) for r in range(R1)]
        st1 = sb("st1", [P, NT, 6])
        meanvar1 = sb("meanvar1", [P, NT, 2])
        vareps1 = sb("vareps1", [P, NT])
        negmean1 = sb("negmean1", [P, NT])
        norm1s = [sb(f"norm1s{r}", [P, NT, 2]) for r in range(R1)]
        xn = [sb(f"xn{r}", [P, NT, D]) for r in range(R1)]
        xnT = [sb(f"xnT{r}", [P, S]) for r in range(R1)]
        xsum = [sb(f"xsum{r}", [P, 1]) for r in range(R1)]
        qT = [sb(f"qT{r}", [P, S]) for r in range(R1)]
        zmask = [sb(f"zmask{r}", [P, S]) for r in range(2)]
        negs = [sb(f"negs{r}", [P, S]) for r in range(2)]
        negmax = [sb(f"negmax{r}", [P, NT]) for r in range(R1)]
        probs = [sb(f"probs{r}", [P, SW]) for r in range(R1)]
        psums = [sb(f"psums{r}", [P, NT]) for r in range(R1)]
        probsT = [sb(f"probsT{m}", [P, S]) for m in range(NT)]
        zT = sb("zT", [P, S])
        vtot = [sb(f"vtot{r}", [P, D]) for r in range(R1)]
        u512 = [sb(f"u512_{r}", [P, NT]) for r in range(R1)]
        resid = [sb(f"resid{r}", [P, NT, D]) for r in range(R1)]
        rsum = sb("rsum", [P, NT])
        rlive = sb("rlive", [P, NT])
        row = [sb(f"row{r}", [P, NT, RW]) for r in range(R1)]
        st2 = sb("st2", [P, NT, 6])
        meanvar2 = sb("meanvar2", [P, NT, 2])
        vareps2 = sb("vareps2", [P, NT])
        xn2 = [sb(f"xn2_{r}", [P, NT, D]) for r in range(R1)]
        x2T = sb("x2T", [P, S])
        elog = sb("elog", [P, NT, NL])
        elog1 = sb("elog1", [P, NT, NL])
        sig = sb("sig", [P, NT, NL])
        top = sb("top", [P, NT])
        istop = sb("istop", [P, NT, G])
        rank = sb("rank", [P, NT, G])
        toprank = sb("toprank", [P, NT])
        pick = [sb(f"pick{r}", [P, NT, G], F16) for r in range(R1)]
        micro = sb("micro", [P, NT, G, EPG])
        msel = sb("msel", [P, NT, EPG])
        msum = sb("msum", [P, NT])
        tope = sb("tope", [P, NT])
        wden = sb("wden", [P, NT])
        wrec = sb("wrec", [P, NT])
        wtop = sb("wtop", [P, NT])
        four = sb("four", [P, G], F16)
        carry = [sb(f"carry{r}", [P, G], F16) for r in range(R1)]
        posm = sb("posm", [P, NT, G])
        place = [sb(f"place{r}", [P, NT], I32) for r in range(R1)]
        ends = sb("ends", [1, G])
        padat = sb("padat", [1, G], I32)
        tileat = sb("tileat", [1, G, T // P])
        tilehit = sb("tilehit", [1, G, T // P])
        tiles = sb("tiles", [1, G])
        tcum = sb("tcum", [1, G])
        skip = sb("skip", [1, G])
        slotno = sb("slotno", [1, G, SLOTS])
        past = sb("past", [1, G, SLOTS])
        pastskip = sb("pastskip", [1, G, SLOTS])
        grp_f = sb("grp_f", [1, SLOTS])
        rowsum = sb("rowsum", [1, SLOTS])
        slot_group = sb("slot_group", [1, SLOTS], I32)
        slot_row = sb("slot_row", [1, SLOTS], I32)
        rowin = [sb(f"rowin{r}", [P, RW]) for r in range(R2)]
        yn = [sb(f"yn{r}", [P, D]) for r in range(R2)]
        yh = [sb(f"yh{r}", [P, P], F32R) for r in range(2)]
        yl = [sb(f"yl{r}", [P, P], F32R) for r in range(2)]
        silu_first = sb("silu_first", [P, 1])
        act_g = [sb(f"act_g{r}", [P, EF]) for r in range(2)]
        hid = [sb(f"hid{r}", [P, EF]) for r in range(2)]
        hh = [sb(f"hh{r}", [P, EF], F32R) for r in range(2)]
        hl = [sb(f"hl{r}", [P, EF], F32R) for r in range(2)]
        outx = sb("outx", [P, D])
        outb = [sb(f"outb{r}", [P, D]) for r in range(R2)]

        bank = [ctx.enter_context(nc.psum_tensor(f"bank{i}", [P, 512], F32)) for i in range(8)]
        ps_tr, ps_z, ps_o, ps_m = bank[0], bank[1], bank[6], bank[7]
        ps_s, ps_pt = bank[2:4], bank[4:6]
        ps_vtot = ps_m[:, 0:D]
        ps_log = ps_m[:, D:D + NT * NL].rearrange("p (i l) -> p i l", l=NL)
        ps_pos = ps_m[:, 192:192 + NT * G].rearrange("p (i g) -> p i g", g=G)
        ps_end = ps_m[:, 256:256 + G]
        ps_y, ps_g, ps_u, ps_ht, ps_out = bank[0], bank[1:3], bank[3:5], bank[5], bank[6]

        w_in = sem("w_in")
        r_in = sem("r_in")
        e_in = [sem(f"e_in{g}") for g in range(G)]
        pad_out = sem("pad_out")
        x_in = [sem(f"x_in{r}") for r in range(R1)]
        res_in = [sem(f"res_in{r}") for r in range(R1)]
        scattered = [sem(f"scattered{r}") for r in range(R1)]
        consts = sem("consts")
        waits_passed = sem("waits_passed")
        wT_ready = sem("wT_ready")
        wT_done = sem("wT_done")
        wqk_ready = sem("wqk_ready")
        wqk_done = sem("wqk_done")
        wh_done = sem("wh_done")
        wl_done = sem("wl_done")
        ln1_stats = sem("ln1_stats")
        rstd1 = sem("rstd1")
        rstd2 = sem("rstd2")
        tokens_noted = sem("tokens_noted")
        ln1_norm = sem("ln1_norm")
        xT_ready = sem("xT_ready")
        xT_done = sem("xT_done")
        q_ready = sem("q_ready")
        q_done = sem("q_done")
        s_ready = sem("s_ready")
        zero_found = sem("zero_found")
        s_masked = sem("s_masked")
        p_done = sem("p_done")
        pT_ready = sem("pT_ready")
        pT_done = sem("pT_done")
        z_ready = sem("z_ready")
        z_done = sem("z_done")
        vt_ready = sem("vt_ready")
        vt_done = sem("vt_done")
        o_ready = sem("o_ready")
        masked_found = sem("masked_found")
        resid_step = sem("resid_step")
        x1_step = sem("x1_step")
        ln2_norm = sem("ln2_norm")
        x2T_ready = sem("x2T_ready")
        x2T_done = sem("x2T_done")
        log_ready = sem("log_ready")
        exp_done = sem("exp_done")
        route = sem("route")
        counted = sem("counted")
        pos_ready = sem("pos_ready")
        place_step = sem("place_step")
        end_ready = sem("end_ready")
        table = sem("table")
        padded = sem("padded")
        numbered = sem("numbered")
        slots_numbered = sem("slots_numbered")
        rows_in = [sem(f"rows_in{r}") for r in range(R2)]
        yn_done = sem("yn_done")
        yT_ready = sem("yT_ready")
        yh_done = sem("yh_done")
        yl_done = sem("yl_done")
        g_ready = sem("g_ready")
        u_ready = sem("u_ready")
        silu_done = sem("silu_done")
        h_done = sem("h_done")
        hT_ready = sem("hT_ready")
        hh_done = sem("hh_done")
        hl_done = sem("hl_done")
        y_ready = sem("y_ready")
        out_part = sem("out_part")
        out_done = sem("out_done")
        out_sent = [sem(f"out_sent{r}") for r in range(R2)]

        N_CONST = 9
        LN1, RES, X1, LN2, ROUTE, COUNT, RSTD1, RSTD2 = 4, 2, 14, 4, 15, 2, 4, 3
        TABLE = 12

        x_v = x_d.rearrange("b (i p) d -> b p i d", p=P)

        block = ctx.enter_context(nc.Block())

        def end_waits(eng):
            eng.sem_inc(waits_passed, 1)

        def attention_steps(eng, step):
            for k in STEPS[0]:
                step(Turn(R1, 0, k))
            with eng.Fori(*STEPS[1]) as trip:
                for r in range(R1):
                    step(Turn(R1, trip, r))
            for k in STEPS[2]:
                step(Turn(R1, 0, k))

        def live(k, late):
            return not isinstance(k.trip, int) or 0 <= k.off - late < B

        def expert_steps(eng, step):
            for s in range(-1, R2 + 2):
                step(Turn(R2, 0, s))
            with eng.Fori(1, 8) as trip:
                for r in range(R2):
                    step(Turn(R2, trip, 2 + r))
            for s in range(SLOTS - 1, SLOTS + 2):
                step(Turn(R2, 0, s))

        def slot_live(s, late):
            return not isinstance(s.trip, int) or 0 <= s.off - late < SLOTS

        @block.sync
        def _(sp):
            def load_x(n):
                if n.has(R1):
                    sp.wait_ge(ln1_norm, (n - R1).count(LN1, LN1))
                sp.dma_start(xin[n.buf][:, :, :], x_v[bass.ds(n.number, 1), :, :, :].rearrange("b p i d -> (b p) i d")
                             if not isinstance(n.trip, int) else x_v[n.off]).then_inc(x_in[n.buf], 16)

            def load_res(n):
                if n.has(R1):
                    sp.wait_ge(resid_step, (n - R1).count(RES, RES))
                sp.dma_start(xres[n.buf][:, :, :], x_v[bass.ds(n.number, 1), :, :, :].rearrange("b p i d -> (b p) i d")
                             if not isinstance(n.trip, int) else x_v[n.off]).then_inc(res_in[n.buf], 16)

            load_x(Turn(R1, 0, 0))
            load_x(Turn(R1, 0, 1))
            load_res(Turn(R1, 0, 0))
            load_x(Turn(R1, 0, 2))
            for g in range(G):
                for v, src in enumerate((gate_d, up_d)):
                    sp.dma_start(wgu[:, g, v * EF:(v + 1) * EF].rearrange("p (e f) -> p e f", f=F),
                                 src[g * EPG:(g + 1) * EPG].rearrange("e p f -> p e f")).then_inc(e_in[g], 16)
                sp.dma_start(wd[:, g, :, :], down_d[g * EPG:(g + 1) * EPG].rearrange(
                    "e (c p) d -> p (e c) d", p=P)).then_inc(e_in[g], 16)
            sp.wait_ge(numbered, 1)
            for g in range(G - 1):
                sp.dma_start(scratch[G * REGION + g * P:G * REGION + (g + 1) * P, :], padrow[:, :]).then_inc(pad_out, 16)
            load_x(Turn(R1, 0, 3))
            load_res(Turn(R1, 0, 1))
            load_x(Turn(R1, 0, 4))
            load_res(Turn(R1, 0, 2))
            load_x(Turn(R1, 0, 5))
            with sp.Fori(1, 4) as trip:
                for r in range(R1):
                    load_res(Turn(R1, trip, r))
                    load_x(Turn(R1, trip, r + R1))
            for n in range(12, B):
                load_res(Turn(R1, 0, n))
                if n + R1 < B:
                    load_x(Turn(R1, 0, n + R1))

            def load_rows(s):
                if s.has(R2):
                    sp.wait_ge(out_sent[s.buf], (s - R2).round * 16 + 16)
                at = sp.value_load(slot_row[0:1, bass.ds(s.number, 1)], min_val=0, max_val=ROWS - P)
                sp.dma_start(rowin[s.buf][:, :], scratch[bass.ds(at, P), :]).then_inc(rows_in[s.buf], 16)

            sp.wait_ge(table, 1)
            for g in range(G):
                at = sp.value_load(padat[0:1, g:g + 1], min_val=g * REGION, max_val=g * REGION + T)
                sp.dma_start(scratch[bass.ds(at, P), :], padrow[:, :]).then_inc(padded, 16)

            sp.wait_ge(table, TABLE)
            sp.wait_ge(padded, 16 * G)
            sp.wait_ge(pad_out, 16 * (G - 1))
            for r in range(R1):
                sp.wait_ge(scattered[r], 16 * NT * ((B - 1 - r) // R1 + 1))
            for r in range(R2):
                load_rows(Turn(R2, 0, r))
            with sp.Fori(1, 8) as trip:
                for r in range(R2):
                    load_rows(Turn(R2, trip, r))
            for s in range(8 * R2, SLOTS):
                load_rows(Turn(R2, 0, s))

        @block.gpsimd
        def _(pool):
            for t in (ident, identb):
                nc.gpsimd.memset(t[:, :], 0.0).then_inc(consts, 1)
            pool.wait_ge(consts, 2)
            for t in (ident, identb):
                nc.gpsimd.affine_select(out=t[:, :], in_=t[:, :], compare_op=ALU.not_equal, fill=1.0, base=0,
                                        pattern=[[-1, P]], channel_multiplier=1).then_inc(consts, 1)
            nc.gpsimd.memset(trineg[:, :], 0.0).then_inc(consts, 1)
            nc.gpsimd.memset(before[:, :], 0.0).then_inc(consts, 1)
            pool.wait_ge(consts, 6)
            nc.gpsimd.affine_select(out=trineg[:, :], in_=trineg[:, :], compare_op=ALU.is_ge, fill=MASKED, base=0,
                                    pattern=[[1, P]], channel_multiplier=-1).then_inc(consts, 1)
            nc.gpsimd.affine_select(out=before[:, :], in_=before[:, :], compare_op=ALU.is_ge, fill=1.0, base=0,
                                    pattern=[[-1, P]], channel_multiplier=1).then_inc(consts, 1)
            nc.gpsimd.memset(ones[:, :], 1.0)
            nc.gpsimd.memset(halfneg[:, :], -0.5)
            for g in range(G):
                nc.gpsimd.memset(prefer[:, :, g], float(G - g))
                nc.gpsimd.memset(carry[0][:, g:g + 1], float(g * REGION // P))
            nc.gpsimd.memset(padrow[:, :], 0.0)
            for r in range(R1):
                last = nc.gpsimd.memset(row[r][:, :, RW - 4:RW], 0.0)
            last.then_inc(consts, 1)
            pool.wait_ge(consts, N_CONST)
            for r in range(R1):
                nc.gpsimd.iota(row[r][:, :, TOKEN].bitcast(I32), pattern=[[P, NT]], base=(r - R1) * S,
                               channel_multiplier=1)
            nc.gpsimd.iota(padrow[:, TOKEN:TOKEN + 1].bitcast(I32), pattern=[[0, 1]], base=T,
                           channel_multiplier=0).then_inc(numbered, 1)

            def deviations1(n):
                pool.wait_ge(ln1_stats, n.count(2 * NT, 2 * NT))
                if n.has(1):
                    pool.wait_ge(rstd1, n.count(RSTD1, 0))
                end_waits(pool)
                nc.gpsimd.tensor_scalar(vareps1[:, :], meanvar1[:, :, 1], LN_EPS, None, ALU.add).then_inc(rstd1, 1)
                nc.gpsimd.tensor_scalar(negmean1[:, :], meanvar1[:, :, 0], -1.0, None, ALU.mult).then_inc(rstd1, 1)
                pool.wait_ge(rstd1, n.count(RSTD1, 1))
                nc.gpsimd.tensor_tensor(norm1s[n.buf][:, :, 1], vareps1[:, :], halfneg[:, :], ALU.pow).then_inc(rstd1, 1)
                pool.wait_ge(rstd1, n.count(RSTD1, 3))
                nc.gpsimd.tensor_tensor(norm1s[n.buf][:, :, 0], negmean1[:, :], norm1s[n.buf][:, :, 1],
                                        ALU.mult).then_inc(rstd1, 1)

            def deviations2(n):
                pool.wait_ge(x1_step, n.count(X1, X1))
                if n.has(1):
                    pool.wait_ge(rstd2, n.count(RSTD2, 0))
                end_waits(pool)
                nc.gpsimd.tensor_scalar(vareps2[:, :], meanvar2[:, :, 1], LN_EPS, None, ALU.add).then_inc(rstd2, 1)
                nc.gpsimd.tensor_scalar(row[n.buf][:, :, NEGMEAN], meanvar2[:, :, 0], -1.0, None, ALU.mult).then_inc(rstd2, 1)
                pool.wait_ge(rstd2, n.count(RSTD2, 1))
                nc.gpsimd.tensor_tensor(row[n.buf][:, :, RSTD], vareps2[:, :], halfneg[:, :], ALU.pow).then_inc(rstd2, 1)

            def scatter(n):
                pool.wait_ge(place_step, n.count(2, 2))
                pool.wait_ge(route, n.count(ROUTE, ROUTE))
                pool.wait_ge(tokens_noted, n.count(1, 1))
                pool.wait_ge(rstd2, n.count(RSTD2, RSTD2))
                end_waits(pool)
                for i in range(NT):
                    nc.gpsimd.indirect_dma_start(
                        out=scratch, out_offset=bass.IndirectOffsetOnAxis(ap=place[n.buf][:, i:i + 1], axis=0),
                        in_=row[n.buf][:, i, :], in_offset=None).then_inc(scattered[n.buf], 16)

            def residual(n):
                pool.wait_ge(masked_found, n.count(1, 1))
                pool.wait_ge(vt_done, n.count(1, 1))
                if n.has(R1):
                    pool.wait_ge(x1_step, (n - R1).count(X1, X1))
                nc.gpsimd.tensor_tensor(resid[n.buf][:, :, :], vtot[n.buf][:, None, :].to_broadcast([P, NT, D]),
                                        u512[n.buf][:, :, None].to_broadcast([P, NT, D]), ALU.mult).then_inc(resid_step, 1)
                pool.wait_ge(res_in[n.buf], n.round * 16 + 16)
                pool.wait_ge(resid_step, n.count(RES, 1))
                nc.gpsimd.tensor_tensor(resid[n.buf][:, :, :], resid[n.buf][:, :, :], xres[n.buf][:, :, :],
                                        ALU.add).then_inc(resid_step, 1)

            def step(k):
                if live(k, 3):
                    deviations2(k - 3)
                if live(k, 2):
                    residual(k - 2)
                if live(k, -2):
                    deviations1(k + 2)
                if live(k, 4):
                    scatter(k - 4)
                if isinstance(k.trip, int) and k.off == 1:
                    nc.gpsimd.iota(tileat[:, :, :], pattern=[[REGION, G], [P, T // P]], base=0, channel_multiplier=0,
                                   allow_small_or_imprecise_dtypes=True)
                    nc.gpsimd.iota(slotno[:, :, :], pattern=[[0, G], [1, SLOTS]], base=0, channel_multiplier=0,
                                   allow_small_or_imprecise_dtypes=True).then_inc(slots_numbered, 1)

            attention_steps(pool, step)

            def normalise(s):
                pool.wait_ge(rows_in[s.buf], s.round * 16 + 16)
                if s.has(R2):
                    pool.wait_ge(yT_ready, (s - R2).count(1, 1))
                end_waits(pool)
                rt = rowin[s.buf]
                nc.gpsimd.tensor_scalar(yn[s.buf][:, :], rt[:, 0:D], rt[:, NEGMEAN:NEGMEAN + 1], rt[:, RSTD:RSTD + 1],
                                        ALU.add, ALU.mult).then_inc(yn_done, 1)

            def send(s):
                pool.wait_ge(out_done, s.count(1, 1))
                end_waits(pool)
                nc.gpsimd.indirect_dma_start(
                    out=out_d.rearrange("b s d -> (b s) d"),
                    out_offset=bass.IndirectOffsetOnAxis(ap=rowin[s.buf][:, TOKEN:TOKEN + 1].bitcast(I32), axis=0),
                    in_=outb[s.buf][:, :], in_offset=None, bounds_check=T - 1, oob_is_err=False
                ).then_inc(out_sent[s.buf], 16)

            AHEAD = 5
            for s in range(AHEAD):
                normalise(Turn(R2, 0, s))
            for s in range(R2 - AHEAD):
                normalise(Turn(R2, 0, s + AHEAD))
                send(Turn(R2, 0, s))
            with pool.Fori(0, 7) as trip:
                for r in range(R2):
                    normalise(Turn(R2, trip, R2 + r))
                    send(Turn(R2, trip, R2 - AHEAD + r))
            for s in range(8 * R2 - AHEAD, SLOTS):
                if s + AHEAD < SLOTS:
                    normalise(Turn(R2, 0, s + AHEAD))
                send(Turn(R2, 0, s))
            for r in range(R2):
                pool.wait_ge(out_sent[r], 16 * ((SLOTS - 1 - r) // R2 + 1))

        @block.scalar
        def _(act):
            act.dma_start(wqkv[:, :], w_d).then_inc(w_in, 16)
            act.dma_start(wrout[:, 0:G], macro_d).then_inc(r_in, 16)
            act.dma_start(wrout[:, G:NL].rearrange("p (g e) -> p g e", e=EPG),
                          micro_d.rearrange("g p e -> p g e")).then_inc(r_in, 16)
            for v, dst in enumerate((wqT, wkT)):
                act.wait_ge(wT_ready, 1)
                nc.scalar.activation(dst[:, :], ps_z[:, v * D:(v + 1) * D], ACT.Copy).then_inc(wT_done, 1)
            act.wait_ge(wqk_ready, 1)
            nc.scalar.activation(wqk[:, :], ps_s[0][:, 0:D], ACT.Copy).then_inc(wqk_done, 1)

            def softmax_exp(n, i):
                act.wait_ge(s_masked, n.count(NT, i + 1))
                nc.scalar.activation(probs[n.buf][:, OFF[i]:OFF[i] + WIDTH[i]], negs[i % 2][:, 0:WIDTH[i]], ACT.Exp,
                                     bias=negmax[n.buf][:, i:i + 1], scale=-1.0,
                                     accum_out=psums[n.buf][:, i:i + 1]).then_inc(p_done, 1)

            def copy_probsT(n, m):
                act.wait_ge(pT_ready, n.count(NT, m + 1))
                w = S - m * P
                nc.scalar.activation(probsT[m][:, 0:w], ps_pt[m % 2][:, 0:w], ACT.Copy).then_inc(pT_done, 1)

            def copy_x2T(n):
                act.wait_ge(x2T_ready, n.count(1, 1))
                nc.scalar.activation(x2T[:, :], ps_tr[:, :], ACT.Copy).then_inc(x2T_done, 1)

            def exp_logits(n):
                act.wait_ge(log_ready, n.count(1, 1))
                if n.has(1):
                    act.wait_ge(route, (n - 1).count(ROUTE, 1))
                nc.scalar.activation(elog[:, :, :], ps_log, ACT.Exp, scale=-1.0).then_inc(exp_done, 1)

            def copy_zT(n):
                act.wait_ge(z_ready, n.count(1, 1))
                nc.scalar.activation(zT[:, :], ps_z[:, :], ACT.Copy).then_inc(z_done, 1)

            def copy_xT(n):
                act.wait_ge(xT_ready, n.count(1, 1))
                nc.scalar.activation(xnT[n.buf][:, :], ps_tr[:, :], ACT.Copy,
                                     accum_out=xsum[n.buf][:, :]).then_inc(xT_done, 1)

            def copy_vtot(n):
                act.wait_ge(vt_ready, n.count(1, 1))
                if n.has(R1):
                    act.wait_ge(resid_step, (n - R1).count(RES, RES))
                nc.scalar.activation(vtot[n.buf][:, :], ps_vtot, ACT.Copy).then_inc(vt_done, 1)

            def upper_weights(g):
                act.wait_ge(e_in[g], 16 * 3)
                nc.scalar.activation(wguh[:, g, :], wgu[:, g, :], ACT.Copy).then_inc(wh_done, 1)
                nc.scalar.activation(wds[:, g, :, 0, :], wd[:, g, :, :], ACT.Copy).then_inc(wh_done, 1)

            def norm1(n, tiles):
                act.wait_ge(rstd1, n.count(RSTD1, RSTD1))
                if n.has(R1):
                    act.wait_ge(z_ready, (n - R1).count(1, 1))
                for i in tiles:
                    nc.scalar.activation(xn[n.buf][:, i, :], xin[n.buf][:, i, :], ACT.Identity,
                                         bias=norm1s[n.buf][:, i, 0:1], scale=norm1s[n.buf][:, i, 1:2]).then_inc(ln1_norm, 1)

            def copy_q(n):
                act.wait_ge(q_ready, n.count(1, 1))
                nc.scalar.activation(qT[n.buf][:, :], ps_o[:, :], ACT.Copy).then_inc(q_done, 1)

            def step(k):
                if isinstance(k.trip, int) and k.off == B + 2:
                    upper_weights(2)
                    upper_weights(3)
                if live(k, 2):
                    copy_probsT(k - 2, 0)
                    copy_probsT(k - 2, 1)
                if live(k, 0):
                    copy_xT(k)
                if live(k, 1):
                    copy_vtot(k - 1)
                    softmax_exp(k - 1, 0)
                if live(k, 2):
                    copy_probsT(k - 2, 2)
                    copy_probsT(k - 2, 3)
                if live(k, 0):
                    copy_q(k)
                if live(k, 2):
                    copy_zT(k - 2)
                if live(k, 3):
                    copy_x2T(k - 3)
                if live(k, 1):
                    softmax_exp(k - 1, 1)
                    softmax_exp(k - 1, 2)
                if live(k, -1):
                    norm1(k + 1, (0, 1))
                if live(k, 3):
                    exp_logits(k - 3)
                if live(k, 1):
                    softmax_exp(k - 1, 3)
                if live(k, -1):
                    norm1(k + 1, (2, 3))
                if isinstance(k.trip, int) and k.off in (0, 1):
                    upper_weights(k.off)

            attention_steps(act, step)

            act.wait_ge(consts, N_CONST)
            nc.scalar.activation(silu_first[:, :], ones[:, 0:1], ACT.Silu)

            def step2(s):
                if slot_live(s, -1):
                    n = s + 1
                    act.wait_ge(yT_ready, n.count(1, 1))
                    if n.has(2):
                        act.wait_ge(u_ready, (n - 2).count(1, 1))
                    nc.scalar.activation(yh[n.buf % 2][:, :], ps_y[:, 0:P], ACT.Copy).then_inc(yh_done, 1)
                if slot_live(s, 0):
                    act.wait_ge(g_ready, s.count(1, 1))
                    if s.has(2):
                        act.wait_ge(h_done, (s - 2).count(EPG, EPG))
                    nc.scalar.activation(act_g[s.buf % 2][:, :], ps_g[s.buf % 2][:, :], ACT.Silu).then_inc(silu_done, 1)
                if slot_live(s, 1):
                    n = s - 1
                    act.wait_ge(hT_ready, n.count(1, 1))
                    if n.has(2):
                        act.wait_ge(y_ready, (n - 2).count(1, 1))
                    nc.scalar.activation(hh[n.buf % 2][:, :], ps_ht[:, :], ACT.Copy).then_inc(hh_done, 1)

            expert_steps(act, step2)

        @block.vector
        def _(dve):
            def position_of_pick(n):
                dve.wait_ge(pos_ready, n.count(1, 1))
                nc.vector.tensor_tensor(posm[:, :, :], ps_pos, pick[n.buf][:, :, :], ALU.mult).then_inc(place_step, 1)

            def place_rows(n):
                dve.wait_ge(place_step, n.count(2, 1))
                with nc.allow_low_precision(reason="whole numbers below 2**24, summed in float32"):
                    nc.vector.tensor_reduce(out=place[n.buf][:, :], in_=posm[:, :, :], op=ALU.add,
                                            axis=AX.X).then_inc(place_step, 1)

            def find_zeros(n, i):
                dve.wait_ge(s_ready, n.count(NT, i + 1))
                w = WIDTH[i]
                nc.vector.tensor_scalar(zmask[i % 2][:, 0:w], ps_s[i % 2][:, 0:w], 0.0, MASKED, ALU.is_equal,
                                        ALU.mult).then_inc(zero_found, 1)

            def mask_scores(n, i):
                w = WIDTH[i]
                dve.wait_ge(zero_found, n.count(NT, i + 1))
                if n.has(1) or i >= 2:
                    dve.wait_ge(p_done, n.count(NT, i - 1))
                end_waits(dve)
                nc.vector.tensor_tensor_reduce(out=negs[i % 2][:, 0:w], in0=ps_s[i % 2][:, 0:w],
                                               in1=zmask[i % 2][:, 0:w], scale=-SCALE, scalar=3.0e38,
                                               op0=ALU.add, op1=ALU.min,
                                               accum_out=negmax[n.buf][:, i:i + 1]).then_inc(s_masked, 1)

            def find_masked(n):
                dve.wait_ge(s_masked, n.count(NT, NT))
                if n.has(R1):
                    dve.wait_ge(resid_step, (n - R1).count(RES, 1))
                nc.vector.tensor_scalar(u512[n.buf][:, :], negmax[n.buf][:, :], ALL_MASKED, 1.0 / S, ALU.is_gt,
                                        ALU.mult).then_inc(masked_found, 1)

            def count_batch(n):
                dve.wait_ge(route, n.count(ROUTE, 7))
                with nc.allow_low_precision(reason="whole numbers below 2048"):
                    nc.vector.tensor_reduce(out=four[:, :], in_=pick[n.buf][:, :, :].rearrange("p i g -> p g i"),
                                            op=ALU.add, axis=AX.X).then_inc(counted, 1)

            def add_count(n):
                dve.wait_ge(counted, n.count(COUNT, 1))
                nc.vector.tensor_tensor(carry[(n + 1).buf][:, :], carry[n.buf][:, :], four[:, :], ALU.add).then_inc(counted, 1)

            def stats1(n, i):
                if i == 0:
                    dve.wait_ge(x_in[n.buf], n.round * 16 + 16)
                    if n.has(1):
                        dve.wait_ge(ln1_stats, n.count(2 * NT, 0))
                nc.vector.bn_stats(st1[:, i, :], xin[n.buf][:, i, :]).then_inc(ln1_stats, 1)

            def meanvar_1(n, i):
                if i == 0:
                    dve.wait_ge(ln1_stats, n.count(2 * NT, NT))
                    if n.has(1):
                        dve.wait_ge(rstd1, (n - 1).count(RSTD1, 2))
                    end_waits(dve)
                nc.vector.bn_aggr(meanvar1[:, i, :], st1[:, i, :]).then_inc(ln1_stats, 1)

            def norm2(n, i):
                if i == 0:
                    dve.wait_ge(rstd2, n.count(RSTD2, RSTD2))
                    if n.has(R1):
                        dve.wait_ge(x2T_ready, (n - R1).count(1, 1))
                nc.vector.tensor_scalar(xn2[n.buf][:, i, :], row[n.buf][:, i, 0:D], row[n.buf][:, i, NEGMEAN:NEGMEAN + 1],
                                        row[n.buf][:, i, RSTD:RSTD + 1], ALU.add, ALU.mult).then_inc(ln2_norm, 1)

            def softmax_reciprocal(n):
                dve.wait_ge(p_done, n.count(NT, NT))
                nc.vector.reciprocal(rsum[:, :], psums[n.buf][:, :]).then_inc(x1_step, 1)

            def live_reciprocal(n):
                dve.wait_ge(x1_step, n.count(X1, 1))
                nc.vector.scalar_tensor_tensor(out=rlive[:, :], in0=negmax[n.buf][:, :], scalar=ALL_MASKED,
                                               in1=rsum[:, :], op0=ALU.is_le, op1=ALU.mult).then_inc(x1_step, 1)

            def note_tokens(n):
                if n.has(R1):
                    dve.wait_ge(scattered[n.buf], (n - R1).round * 16 * NT + 16 * NT)
                end_waits(dve)
                ids = row[n.buf][:, :, TOKEN].bitcast(I32)
                nc.vector.tensor_scalar(ids, ids, float(R1 * S), None, ALU.add).then_inc(tokens_noted, 1)

            def new_x(n, i):
                if i == 0:
                    dve.wait_ge(x1_step, n.count(X1, 2))
                    dve.wait_ge(resid_step, n.count(RES, RES))
                    dve.wait_ge(o_ready, n.count(1, 1))
                nc.vector.scalar_tensor_tensor(out=row[n.buf][:, i, 0:D], in0=ps_o[:, i * D:(i + 1) * D],
                                               scalar=rlive[:, i:i + 1], in1=resid[n.buf][:, i, :],
                                               op0=ALU.mult, op1=ALU.add).then_inc(x1_step, 1)

            def stats2(n, i):
                if i == 0:
                    dve.wait_ge(x1_step, n.count(X1, 2 + NT))
                nc.vector.bn_stats(st2[:, i, :], row[n.buf][:, i, 0:D]).then_inc(x1_step, 1)

            def meanvar_2(n, i):
                if i == 0:
                    dve.wait_ge(x1_step, n.count(X1, 2 + 2 * NT))
                    if n.has(1):
                        dve.wait_ge(rstd2, (n - 1).count(RSTD2, 2))
                    end_waits(dve)
                nc.vector.bn_aggr(meanvar2[:, i, :], st2[:, i, :]).then_inc(x1_step, 1)

            def sigmoid_denominator(n):
                dve.wait_ge(exp_done, n.count(1, 1))
                nc.vector.tensor_scalar(elog1[:, :, :], elog[:, :, :], 1.0, None, ALU.add).then_inc(route, 1)

            def sigmoid(n):
                dve.wait_ge(route, n.count(ROUTE, 1))
                nc.vector.reciprocal(sig[:, :, :], elog1[:, :, :]).then_inc(route, 1)

            def top_score(n):
                dve.wait_ge(route, n.count(ROUTE, 2))
                nc.vector.tensor_reduce(out=top[:, :], in_=sig[:, :, 0:G], op=ALU.max, axis=AX.X).then_inc(route, 1)

            def groups_at_top(n):
                dve.wait_ge(route, n.count(ROUTE, 3))
                nc.vector.tensor_tensor(istop[:, :, :], sig[:, :, 0:G], top[:, :, None].to_broadcast([P, NT, G]),
                                        ALU.is_equal).then_inc(route, 1)

            def rank_groups(n):
                dve.wait_ge(route, n.count(ROUTE, 4))
                nc.vector.tensor_tensor(rank[:, :, :], istop[:, :, :], prefer[:, :, :], ALU.mult).then_inc(route, 1)

            def top_rank(n):
                dve.wait_ge(route, n.count(ROUTE, 5))
                nc.vector.tensor_reduce(out=toprank[:, :], in_=rank[:, :, :], op=ALU.max, axis=AX.X).then_inc(route, 1)

            def pick_group(n):
                dve.wait_ge(route, n.count(ROUTE, 6))
                nc.vector.tensor_tensor(pick[n.buf][:, :, :], rank[:, :, :],
                                        toprank[:, :, None].to_broadcast([P, NT, G]), ALU.is_equal).then_inc(route, 1)

            def micro_of_pick(n):
                dve.wait_ge(route, n.count(ROUTE, 7))
                nc.vector.tensor_tensor(micro[:, :, :, :], sig[:, :, G:NL].rearrange("p i (g e) -> p i g e", e=EPG),
                                        pick[n.buf][:, :, :, None].to_broadcast([P, NT, G, EPG]),
                                        ALU.mult).then_inc(route, 1)
                nc.vector.tensor_scalar(tope[:, :], top[:, :], TOP_EPS, None, ALU.add).then_inc(route, 1)

            def micro_scores(n):
                dve.wait_ge(route, n.count(ROUTE, 9))
                nc.vector.tensor_reduce(out=msel[:, :, :], in_=micro[:, :, :, :].rearrange("p i g e -> p i e g"),
                                        op=ALU.add, axis=AX.X).then_inc(route, 1)

            def micro_sum(n):
                dve.wait_ge(route, n.count(ROUTE, 10))
                nc.vector.tensor_tensor(msum[:, :], msel[:, :, 0], msel[:, :, 1], ALU.add).then_inc(route, 1)

            def weight_denominator(n):
                dve.wait_ge(route, n.count(ROUTE, 11))
                nc.vector.scalar_tensor_tensor(out=wden[:, :], in0=msum[:, :], scalar=TOP_EPS, in1=tope[:, :],
                                               op0=ALU.add, op1=ALU.mult).then_inc(route, 1)

            def weight_reciprocal(n):
                dve.wait_ge(route, n.count(ROUTE, 12))
                nc.vector.reciprocal(wrec[:, :], wden[:, :]).then_inc(route, 1)

            def weight_factor(n):
                dve.wait_ge(route, n.count(ROUTE, 13))
                nc.vector.tensor_tensor(wtop[:, :], wrec[:, :], top[:, :], ALU.mult).then_inc(route, 1)

            def weights(n):
                dve.wait_ge(route, n.count(ROUTE, 14))
                nc.vector.tensor_tensor(row[n.buf][:, :, WGT:WGT + EPG], msel[:, :, :],
                                        wtop[:, :, None].to_broadcast([P, NT, EPG]), ALU.mult).then_inc(route, 1)

            def lower_weights(g):
                dve.wait_ge(wh_done, 2 * g + 1)
                nc.vector.tensor_tensor(wgul[:, g, :], wgu[:, g, :], wguh[:, g, :].bitcast(F32),
                                        ALU.subtract).then_inc(wl_done, 1)
                dve.wait_ge(wh_done, 2 * g + 2)
                nc.vector.tensor_tensor(wds[:, g, :, 1, :], wd[:, g, :, :], wds[:, g, :, 0, :].bitcast(F32),
                                        ALU.subtract).then_inc(wl_done, 1)

            def step(k):
                if isinstance(k.trip, int) and k.off == 0:
                    dve.wait_ge(consts, N_CONST)
                    dve.wait_ge(numbered, 1)
                if live(k, 4):
                    sigmoid_denominator(k - 4)
                if live(k, -2):
                    stats1(k + 2, 0)
                if live(k, 4):
                    sigmoid(k - 4)
                if live(k, -2):
                    stats1(k + 2, 1)
                if live(k, 4):
                    top_score(k - 4)
                if live(k, -2):
                    stats1(k + 2, 2)
                if live(k, 4):
                    groups_at_top(k - 4)
                if live(k, -2):
                    stats1(k + 2, 3)
                if live(k, 4):
                    rank_groups(k - 4)
                if live(k, 1):
                    find_zeros(k - 1, 0)
                if live(k, 4):
                    top_rank(k - 4)
                if live(k, -2):
                    meanvar_1(k + 2, 0)
                    meanvar_1(k + 2, 1)
                if live(k, 1):
                    mask_scores(k - 1, 0)
                if live(k, 4):
                    pick_group(k - 4)
                if live(k, -2):
                    meanvar_1(k + 2, 2)
                    meanvar_1(k + 2, 3)
                if live(k, 4):
                    count_batch(k - 4)
                if live(k, 3):
                    norm2(k - 3, 0)
                if live(k, 4):
                    micro_of_pick(k - 4)
                if live(k, 3):
                    norm2(k - 3, 1)
                if live(k, 4):
                    micro_scores(k - 4)
                if live(k, 3):
                    norm2(k - 3, 2)
                if live(k, 4):
                    add_count(k - 4)
                    micro_sum(k - 4)
                if live(k, 3):
                    norm2(k - 3, 3)
                if live(k, 4):
                    weight_denominator(k - 4)
                if live(k, 1):
                    find_zeros(k - 1, 1)
                if live(k, 4):
                    weight_reciprocal(k - 4)
                    position_of_pick(k - 4)
                    weight_factor(k - 4)
                if live(k, 1):
                    mask_scores(k - 1, 1)
                if live(k, 4):
                    weights(k - 4)
                    place_rows(k - 4)
                if live(k, 1):
                    find_zeros(k - 1, 2)
                if live(k, 2):
                    softmax_reciprocal(k - 2)
                    live_reciprocal(k - 2)
                if live(k, 1):
                    mask_scores(k - 1, 2)
                if live(k, 2):
                    note_tokens(k - 2)
                    new_x(k - 2, 0)
                if live(k, 1):
                    find_zeros(k - 1, 3)
                if live(k, 2):
                    new_x(k - 2, 1)
                    new_x(k - 2, 2)
                    new_x(k - 2, 3)
                if live(k, 1):
                    mask_scores(k - 1, 3)
                if live(k, 2):
                    for i in range(NT):
                        stats2(k - 2, i)
                if live(k, 1):
                    find_masked(k - 1)
                if live(k, 2):
                    for i in range(NT):
                        meanvar_2(k - 2, i)
                if isinstance(k.trip, int) and k.off in (0, 1):
                    lower_weights(k.off)

            attention_steps(dve, step)

            def after(done):
                dve.wait_ge(table, done)

            dve.wait_ge(end_ready, 1)
            dve.wait_ge(slots_numbered, 1)
            nc.vector.tensor_copy(padat[:, :], ps_end[0:1, :]).then_inc(table, 1)
            nc.vector.tensor_copy(ends[:, :], ps_end[0:1, :]).then_inc(table, 1)
            after(2)
            nc.vector.tensor_tensor(tilehit[:, :, :], tileat[:, :, :], ends[:, :, None].to_broadcast([1, G, T // P]),
                                    ALU.is_lt).then_inc(table, 1)
            after(3)
            nc.vector.tensor_reduce(out=tiles[:, :], in_=tilehit[:, :, :], op=ALU.add, axis=AX.X).then_inc(table, 1)
            after(4)
            nc.vector.tensor_scalar(skip[:, :], tiles[:, :], -float(P), float(REGION), ALU.mult, ALU.add).then_inc(table, 1)
            nc.vector.tensor_tensor_scan(out=tcum[:, :], data0=ones[0:1, 0:G], data1=tiles[:, :], initial=0.0,
                                         op0=ALU.mult, op1=ALU.add).then_inc(table, 1)
            after(6)
            nc.vector.tensor_tensor(past[:, :, :], slotno[:, :, :], tcum[:, :, None].to_broadcast([1, G, SLOTS]),
                                    ALU.is_ge).then_inc(table, 1)
            after(7)
            nc.vector.tensor_tensor(pastskip[:, :, :], past[:, :, :], skip[:, :, None].to_broadcast([1, G, SLOTS]),
                                    ALU.mult).then_inc(table, 1)
            nc.vector.tensor_reduce(out=grp_f[:, :], in_=past[:, :, :].rearrange("p g s -> p s g"), op=ALU.add,
                                    axis=AX.X).then_inc(table, 1)
            after(9)
            nc.vector.tensor_scalar(slot_group[:, :], grp_f[:, :], float(G - 1), None, ALU.min).then_inc(table, 1)
            nc.vector.tensor_reduce(out=rowsum[:, :], in_=pastskip[:, :, :].rearrange("p g s -> p s g"), op=ALU.add,
                                    axis=AX.X).then_inc(table, 1)
            after(11)
            nc.vector.scalar_tensor_tensor(out=slot_row[:, :], in0=slotno[:, 0, :], scalar=float(P), in1=rowsum[:, :],
                                           op0=ALU.mult, op1=ALU.add).then_inc(table, 1)
            lower_weights(2)
            lower_weights(3)

            def step2(s):
                if slot_live(s, -1):
                    n = s + 1
                    dve.wait_ge(yh_done, n.count(1, 1))
                    nc.vector.tensor_tensor(yl[n.buf % 2][:, :], ps_y[:, 0:P], yh[n.buf % 2][:, :].bitcast(F32),
                                            ALU.subtract).then_inc(yl_done, 1)
                if slot_live(s, 1):
                    n = s - 1
                    dve.wait_ge(hh_done, n.count(1, 1))
                    nc.vector.tensor_tensor(hl[n.buf % 2][:, :], ps_ht[:, :], hh[n.buf % 2][:, :].bitcast(F32),
                                            ALU.subtract).then_inc(hl_done, 1)
                if slot_live(s, 0):
                    dve.wait_ge(silu_done, s.count(1, 1))
                    dve.wait_ge(u_ready, s.count(1, 1))
                    if s.has(2):
                        dve.wait_ge(hT_ready, (s - 2).count(1, 1))
                    for e in range(EPG):
                        nc.vector.scalar_tensor_tensor(
                            out=hid[s.buf % 2][:, e * F:(e + 1) * F], in0=act_g[s.buf % 2][:, e * F:(e + 1) * F],
                            scalar=rowin[s.buf][:, WGT + e:WGT + e + 1], in1=ps_u[s.buf % 2][:, e * F:(e + 1) * F],
                            op0=ALU.mult, op1=ALU.mult).then_inc(h_done, 1)
                if slot_live(s, 2):
                    n = s - 2
                    dve.wait_ge(y_ready, n.count(1, 1))
                    if n.has(R2):
                        dve.wait_ge(out_sent[n.buf], (n - R2).round * 16 + 16)
                    nc.vector.tensor_tensor(outx[:, :], ps_out[:, D:2 * D], rowin[n.buf][:, 0:D], ALU.add).then_inc(out_part, 1)
                    dve.wait_ge(out_part, n.count(1, 1))
                    nc.vector.tensor_tensor(outb[n.buf][:, :], ps_out[:, 0:D], outx[:, :], ALU.add).then_inc(out_done, 1)

            expert_steps(dve, step2)

        @block.tensor
        def _(pe):
            pe.wait_ge(w_in, 16)
            pe.wait_ge(consts, N_CONST)
            nc.tensor.transpose(ps_z[:, 0:D], wqkv[:, 0:D], ident[:, :])
            nc.tensor.transpose(ps_z[:, D:2 * D], wqkv[:, D:2 * D], ident[:, :]).then_inc(wT_ready, 1)
            pe.wait_ge(wT_done, 2)
            nc.tensor.matmul(ps_s[0][:, 0:D], wqT[:, :], wkT[:, :], start=True, stop=True).then_inc(wqk_ready, 1)
            pe.wait_ge(wqk_done, 1)
            pe.wait_ge(r_in, 32)

            def positions(n):
                pe.wait_ge(route, n.count(ROUTE, 7))
                if n.has(1):
                    pe.wait_ge(counted, (n - 1).count(COUNT, COUNT))
                if live(n, -3):
                    pe.wait_ge(vt_done, (n + 3).count(1, 1))
                pk = pick[n.buf]
                nc.tensor.matmul(ps_pos, before[:, :], pk[:, :, :], start=True, stop=False)
                nc.tensor.matmul(ps_pos, ones[:, :], carry[n.buf][:, None, :].to_broadcast([P, NT, G]),
                                 start=False, stop=False)
                for i in range(NT - 1):
                    last = nc.tensor.matmul(ps_pos[:, i + 1:NT, :], ones[:, :],
                                            pk[:, i:i + 1, :].to_broadcast([P, NT - 1 - i, G]),
                                            start=False, stop=i == NT - 2)
                last.then_inc(pos_ready, 1)

            def scores(n, i):
                pe.wait_ge(q_done, n.count(1, 1))
                if n.has(1) or i >= 2:
                    pe.wait_ge(s_masked, n.count(NT, i - 1))
                nc.tensor.matmul(ps_s[i % 2][:, 0:WIDTH[i]], qT[n.buf][:, i * P:(i + 1) * P],
                                 xnT[n.buf][:, i * P:S], start=True, stop=False)
                nc.tensor.matmul(ps_s[i % 2][:, 0:P], identb[:, :], trineg[:, :],
                                 start=False, stop=True).then_inc(s_ready, 1)

            def transpose_probs(n, m):
                pe.wait_ge(p_done, n.count(NT, NT))
                if n.has(1) or m >= 2:
                    pe.wait_ge(pT_done, n.count(NT, m - 1))
                j = NT - 1 - m
                for i in range(j + 1):
                    at = OFF[i] + (j - i) * P
                    last = nc.tensor.transpose(ps_pt[m % 2][:, i * P:(i + 1) * P], probs[n.buf][:, at:at + P], ident[:, :])
                last.then_inc(pT_ready, 1)

            def weigh(n, m):
                pe.wait_ge(pT_done, n.count(NT, m + 1))
                if m == 0 and n.has(1):
                    pe.wait_ge(z_done, n.count(1, 0))
                j = NT - 1 - m
                mm = nc.tensor.matmul(ps_z[:, 0:(j + 1) * P], xn[n.buf][:, j, :], probsT[m][:, 0:(j + 1) * P],
                                      start=m == 0, stop=m == NT - 1)
                if m == NT - 1:
                    mm.then_inc(z_ready, 1)

            def transpose_x2(n):
                pe.wait_ge(ln2_norm, n.count(LN2, LN2))
                if live(n, -3):
                    pe.wait_ge(xT_done, (n + 3).count(1, 1))
                elif n.has(1):
                    pe.wait_ge(x2T_done, n.count(1, 0))
                for i in range(NT):
                    last = nc.tensor.transpose(ps_tr[:, i * P:(i + 1) * P], xn2[n.buf][:, i, :], ident[:, :])
                last.then_inc(x2T_ready, 1)

            def logits(n):
                pe.wait_ge(x2T_done, n.count(1, 1))
                if n.has(1):
                    pe.wait_ge(place_step, (n - 1).count(2, 1))
                else:
                    pe.wait_ge(vt_done, (n + 2).count(1, 1))
                for i in range(NT):
                    last = nc.tensor.matmul(ps_log[:, i, :], x2T[:, i * P:(i + 1) * P], wrout[:, :],
                                            start=True, stop=True)
                last.then_inc(log_ready, 1)

            def transpose_x(n):
                pe.wait_ge(ln1_norm, n.count(LN1, LN1))
                if n.has(4):
                    pe.wait_ge(x2T_done, (n - 4).count(1, 1))
                elif n.has(1):
                    pe.wait_ge(xT_done, n.count(1, 0))
                for i in range(NT):
                    last = nc.tensor.transpose(ps_tr[:, i * P:(i + 1) * P], xn[n.buf][:, i, :], ident[:, :])
                last.then_inc(xT_ready, 1)

            def queries(n):
                pe.wait_ge(xT_done, n.count(1, 1))
                if n.has(3):
                    pe.wait_ge(x1_step, (n - 3).count(X1, 2 + NT))
                elif n.has(1):
                    pe.wait_ge(q_done, n.count(1, 0))
                nc.tensor.matmul(ps_o[:, :], wqk[:, :], xnT[n.buf][:, :], start=True, stop=True).then_inc(q_ready, 1)

            def value_total(n):
                if n.has(3):
                    pe.wait_ge(exp_done, (n - 3).count(1, 1))
                nc.tensor.matmul(ps_vtot, xsum[n.buf][:, 0:1].to_broadcast([P, P]), wqkv[:, 2 * D:3 * D],
                                 start=True, stop=True).then_inc(vt_ready, 1)

            def attend(n):
                pe.wait_ge(z_done, n.count(1, 1))
                if live(n, -2):
                    pe.wait_ge(q_done, (n + 2).count(1, 1))
                else:
                    pe.wait_ge(x1_step, (n - 1).count(X1, 2 + NT))
                for i in range(NT):
                    last = nc.tensor.matmul(ps_o[:, i * D:(i + 1) * D], zT[:, i * P:(i + 1) * P],
                                            wqkv[:, 2 * D:3 * D], start=True, stop=True)
                last.then_inc(o_ready, 1)

            def step(k):
                if live(k, 1):
                    scores(k - 1, 0)
                if live(k, 2):
                    transpose_probs(k - 2, 0)
                    transpose_probs(k - 2, 1)
                if live(k, 0):
                    transpose_x(k)
                if live(k, 1):
                    value_total(k - 1)
                if live(k, 2):
                    weigh(k - 2, 0)
                if live(k, 1):
                    scores(k - 1, 1)
                if live(k, 2):
                    transpose_probs(k - 2, 2)
                    transpose_probs(k - 2, 3)
                    weigh(k - 2, 1)
                if live(k, 0):
                    queries(k)
                if live(k, 2):
                    weigh(k - 2, 2)
                    weigh(k - 2, 3)
                if live(k, 4):
                    positions(k - 4)
                if live(k, 3):
                    transpose_x2(k - 3)
                if live(k, 1):
                    scores(k - 1, 2)
                if live(k, 2):
                    attend(k - 2)
                if live(k, 1):
                    scores(k - 1, 3)
                if live(k, 3):
                    logits(k - 3)

            attention_steps(pe, step)

            pe.wait_ge(counted, B * COUNT)
            pe.wait_ge(place_step, 2 * B)
            nc.tensor.matmul(ps_end, ones[:, :], carry[B % R1][:, :], start=True, stop=True).then_inc(end_ready, 1)

            pe.wait_ge(wl_done, 2 * G)
            pe.wait_ge(table, TABLE)

            def group_of(s):
                return pe.value_load(slot_group[0:1, bass.ds(s.number, 1)], min_val=0, max_val=G - 1)

            def split_matmul(out, hi, lo, whi, wlo, start, stop):
                nc.tensor.matmul(out, hi, whi, start=start, stop=False)
                nc.tensor.matmul(out, hi, wlo, start=False, stop=False)
                return nc.tensor.matmul(out, lo, whi, start=False, stop=stop)

            loaded = {}

            def step2(s):
                if slot_live(s, 0):
                    pe.wait_ge(yl_done, s.count(1, 1))
                    g = loaded[isinstance(s.trip, int), s.off] = group_of(s)
                if slot_live(s, -1):
                    n = s + 1
                    pe.wait_ge(yn_done, n.count(1, 1))
                    nc.tensor.transpose(ps_y[:, 0:P], yn[n.buf][:, :], ident[:, :]).then_inc(yT_ready, 1)
                if slot_live(s, 0):
                    b = s.buf % 2
                    split_matmul(ps_g[b][:, :], yh[b][:, :], yl[b][:, :],
                                 wguh[:, bass.ds(g, 1), 0:EF].rearrange("p g f -> p (g f)"),
                                 wgul[:, bass.ds(g, 1), 0:EF].rearrange("p g f -> p (g f)"),
                                 True, True).then_inc(g_ready, 1)
                if slot_live(s, 2):
                    here = isinstance(s.trip, int), s.off - 2
                    gd = loaded[here] if here in loaded else group_of(s - 2)
                if slot_live(s, 2):
                    pe.wait_ge(hl_done, (s - 2).count(1, 1))
                if slot_live(s, 1):
                    n = s - 1
                    pe.wait_ge(h_done, n.count(EPG, EPG))
                    for c in range(NC):
                        last = nc.tensor.transpose(ps_ht[:, c * P:(c + 1) * P], hid[n.buf % 2][:, c * P:(c + 1) * P],
                                                   ident[:, :])
                    last.then_inc(hT_ready, 1)
                if slot_live(s, 0):
                    split_matmul(ps_u[b][:, :], yh[b][:, :], yl[b][:, :],
                                 wguh[:, bass.ds(g, 1), EF:2 * EF].rearrange("p g f -> p (g f)"),
                                 wgul[:, bass.ds(g, 1), EF:2 * EF].rearrange("p g f -> p (g f)"),
                                 True, True).then_inc(u_ready, 1)
                if slot_live(s, 2):
                    n = s - 2
                    if n.has(1):
                        pe.wait_ge(out_done, n.count(1, 0))
                    for c in range(NC):
                        hi, lo = hh[n.buf % 2][:, c * P:(c + 1) * P], hl[n.buf % 2][:, c * P:(c + 1) * P]
                        wdc = wds[:, bass.ds(gd, 1), c, :, :].rearrange("p g v d -> p (g v) d")
                        if c == NC - 1:
                            nc.tensor.matmul(ps_out[:, 0:D], lo, wdc[:, 0, :], start=False, stop=False)
                        last = nc.tensor.matmul(ps_out[:, 0:2 * D], hi, wdc, start=c == 0, stop=c == NC - 1)
                        if c < NC - 1:
                            nc.tensor.matmul(ps_out[:, 0:D], lo, wdc[:, 0, :], start=False, stop=False)
                    last.then_inc(y_ready, 1)

            expert_steps(pe, step2)


_INS = ['L0_attn_x', 'L0_attn_W', 'L0_ffn_macro_w', 'L0_ffn_micro_w', 'L0_ffn_gate_w', 'L0_ffn_up_w', 'L0_ffn_down_w']
_OUTS = [((16, 512, 128), 'float32')]


def kernel(**inputs):
    import numpy as _np
    import concourse.bacc as _bacc
    from concourse import mybir as _mybir
    from concourse.bass_utils import run_bass_kernel_spmd as _run

    nc = _bacc.Bacc("TRN2", target_bir_lowering=False, num_devices=1)
    arrays, args = {}, []
    for name in _INS:
        a = _np.ascontiguousarray(inputs[name])
        arrays[f"in_{name}_dram"] = a
        args.append(nc.dram_tensor(f"in_{name}_dram", a.shape, _mybir.dt.from_np(a.dtype), kind="ExternalInput").ap())
    for i, (shape, dtype) in enumerate(_OUTS):
        dt = _mybir.dt.from_np(_np.dtype(dtype))
        args.append(nc.dram_tensor(f"out_{i}_dram", shape, dt, kind="ExternalOutput").ap())
    preln_attention_moe_kernel(nc, *args)
    r = _run(nc, [arrays], core_ids=[0])
    got = tuple(r.results[0][f"out_{i}_dram"] for i in range(len(_OUTS)))
    return got[0]
```
